# Optimizing a Trainium2 kernel written in Bass

```python
import numpy as np
import jax
import jax.numpy as jnp

def _softmax(x, axis=-1):
    return jax.nn.softmax(x, axis=axis)

def _gelu(x):
    return jax.nn.gelu(x, approximate=True)

def _silu(x):
    return jax.nn.silu(x)

def _sigmoid(x):
    return jax.nn.sigmoid(x)

def _layernorm(x, axis=-1, eps=1e-05):
    m = jnp.mean(x, axis=axis, keepdims=True)
    v = jnp.var(x, axis=axis, keepdims=True)
    return (x - m) / jnp.sqrt(v + eps)

def _scatter_add(tgt, idx, src, axis=0):
    return tgt.at[idx].add(src)

def _segment_sum(src, seg, n):
    return jax.ops.segment_sum(src, seg, n)
kernel_name = 'mk_decoder_postln_d1_seqx_r8_e9cbe8'

def setup_inputs(seed: int=0):
    np.random.seed(seed)
    _w = jnp.asarray

    def _rec_inputs():
        import jax
        import jax.numpy as jnp
        _rk = jax.random.key(seed)
        x = -0.0002928 + 1 * jax.random.normal(jax.random.fold_in(_rk, 1), (8, 128, 128), jnp.float32)
        _lenS = 128 - jax.random.randint(jax.random.fold_in(_rk, 7), (8,), 0, max(1, 128 // 4) + 1, jnp.int32)
        _lenS2 = 128 - jax.random.randint(jax.random.fold_in(_rk, 8), (8,), 0, max(1, 128 // 4) + 1, jnp.int32)
        _ctx_1024P = jax.random.normal(jax.random.fold_in(_rk, 11), (8, 16, 128), jnp.float32)
        _ctx_1024c = jax.random.dirichlet(jax.random.fold_in(_rk, 511), 0.3 * jnp.ones((16,), jnp.float32), (8, 128))
        _ctx_1024t = jnp.einsum('bsk,bkd->bsd', _ctx_1024c, _ctx_1024P)
        _ctx_1024t = _ctx_1024t * jax.lax.rsqrt(jnp.mean(jnp.square(_ctx_1024t)) + 1e-12) * 0.953939
        ctx_1024 = -1.39393e-06 + 0.999914 * (_ctx_1024t + 0.3 * jax.random.normal(jax.random.fold_in(_rk, 611), (8, 128, 128), jnp.float32))
        return (x, ctx_1024)
    x, ctx_1024 = _rec_inputs()

    def _L0_attn_setup():
        import jax, jax.numpy as jnp
        import numpy as np
        B, N, D = (1, 256, 128)
        H = 16
        HD = D // H
        MAX_REL = 100
        NUM_EMB = 2 * MAX_REL - 1
        NEG = 100000000.0

        def _rel_pos_logits(q_pos, rel_emb):
            L = q_pos.shape[0]
            pad_len = max(L - MAX_REL, 0)
            start = max(MAX_REL - L, 0)
            padded = jnp.pad(rel_emb, ((0, 0), (pad_len, pad_len), (0, 0)))
            used = padded[:, start:start + 2 * L - 1, :]
            q4 = q_pos.reshape(L, -1, H, HD)
            logits = jnp.einsum('lbhd,hmd->lbhm', q4, used)
            logits = logits.reshape(L, -1, 2 * L - 1)
            if pad_len > 0:
                logits = logits.at[:, :, :pad_len].add(-NEG)
                logits = logits.at[:, :, -pad_len:].add(-NEG)
            bh = logits.shape[1]
            x = jnp.pad(logits, ((0, 0), (0, 0), (0, 1)))
            x = jnp.transpose(x, (1, 0, 2)).reshape(bh, L * 2 * L)
            x = jnp.pad(x, ((0, 0), (0, L - 1)))
            x = x.reshape(bh, L + 1, 2 * L - 1)
            return x[:, :L, L - 1:]
        key = jax.random.key(seed)
        ks = jax.random.split(key, 6)
        x = jax.random.normal(ks[0], (B, N, D), dtype=jnp.float32)
        qkv_w = jax.random.normal(ks[1], (3 * D, D), dtype=jnp.float32) * 0.02
        qkv_b = jnp.zeros((3 * D,), dtype=jnp.float32)
        proj_w = jax.random.normal(ks[2], (D, D), dtype=jnp.float32) * 0.02
        proj_b = jnp.zeros((D,), dtype=jnp.float32)
        rel_emb = jax.random.normal(ks[3], (H, NUM_EMB, HD), dtype=jnp.float32) * HD ** (-0.5)
        return {'x': x, 'qkv_w': qkv_w, 'qkv_b': qkv_b, 'proj_w': proj_w, 'proj_b': proj_b, 'rel_emb': rel_emb}
    _L0_attn_all = _L0_attn_setup()
    _L0_attn_in = {k: v for k, v in _L0_attn_all.items() if k in ('qkv_w', 'qkv_b', 'proj_w', 'proj_b', 'rel_emb')}
    del _L0_attn_all

    def _L0_xattn_setup():
        import jax, jax.numpy as jnp
        import numpy as np
        DIM = 128
        N_HEADS = 16
        HEAD_DIM = DIM // N_HEADS
        key = jax.random.key(seed)
        ks = jax.random.split(key, 7)
        B, S = (2, 256)
        scale = 0.02
        return {'q': jax.random.normal(ks[0], (B, S, DIM), dtype=jnp.float32), 'k': jax.random.normal(ks[1], (B, S, DIM), dtype=jnp.float32), 'v': jax.random.normal(ks[2], (B, S, DIM), dtype=jnp.float32), 'wq': jax.random.normal(ks[3], (DIM, DIM), dtype=jnp.float32) * scale, 'wk': jax.random.normal(ks[4], (DIM, DIM), dtype=jnp.float32) * scale, 'wv': jax.random.normal(ks[5], (DIM, DIM), dtype=jnp.float32) * scale, 'wo': jax.random.normal(ks[6], (DIM, DIM), dtype=jnp.float32) * scale}
    _L0_xattn_all = _L0_xattn_setup()
    _L0_xattn_in = {k: v for k, v in _L0_xattn_all.items() if k in ('wq', 'wk', 'wv', 'wo')}
    del _L0_xattn_all

    def _L0_ffn_setup():
        import jax, jax.numpy as jnp
        import numpy as np
        H = 128
        E = 64
        K = 8
        G = 8
        TOPK_GROUP = 4
        I_MOE = 64
        I_SHARED = 256
        SCALE = 2.5

        def relu2(x):
            return jnp.square(jax.nn.relu(x))

        def _route(xf, router_w, correction_bias):
            T = xf.shape[0]
            logits = xf @ router_w.T
            scores = jax.nn.sigmoid(logits)
            sfc = scores + correction_bias[None, :]
            grp = sfc.reshape(T, G, E // G)
            top2, _ = jax.lax.top_k(grp, 2)
            group_scores = top2.sum(-1)
            _, gidx = jax.lax.top_k(group_scores, TOPK_GROUP)
            gmask = jnp.zeros((T, G), sfc.dtype).at[jnp.arange(T)[:, None], gidx].set(1.0)
            emask = jnp.repeat(gmask, E // G, axis=1)
            masked = jnp.where(emask > 0, sfc, 0.0)
            _, tidx = jax.lax.top_k(masked, K)
            tw = jnp.take_along_axis(scores, tidx, axis=1)
            tw = tw / (tw.sum(-1, keepdims=True) + 1e-20)
            return (tidx, tw * SCALE)
        key = jax.random.key(seed)
        ks = jax.random.split(key, 7)
        x = jax.random.normal(ks[0], (2, 128, H), dtype=jnp.float32)
        router_w = jax.random.normal(ks[1], (E, H), dtype=jnp.float32) * 0.02
        correction_bias = jax.random.normal(ks[2], (E,), dtype=jnp.float32) * 0.01
        up_w = jax.random.normal(ks[3], (E, H, I_MOE), dtype=jnp.float32) * 0.02
        down_w = jax.random.normal(ks[4], (E, I_MOE, H), dtype=jnp.float32) * 0.02
        shared_up_w = jax.random.normal(ks[5], (H, I_SHARED), dtype=jnp.float32) * 0.02
        shared_down_w = jax.random.normal(ks[6], (I_SHARED, H), dtype=jnp.float32) * 0.02
        return {'x': x, 'router_w': router_w, 'correction_bias': correction_bias, 'up_w': up_w, 'down_w': down_w, 'shared_up_w': shared_up_w, 'shared_down_w': shared_down_w}
    _L0_ffn_all = _L0_ffn_setup()
    _L0_ffn_in = {k: v for k, v in _L0_ffn_all.items() if k in ('router_w', 'correction_bias', 'up_w', 'down_w', 'shared_up_w', 'shared_down_w')}
    del _L0_ffn_all
    return {'x': x, 'ctx_1024': ctx_1024, 'L0_attn_qkv_w': _L0_attn_in['qkv_w'], 'L0_attn_qkv_b': _L0_attn_in['qkv_b'], 'L0_attn_proj_w': _L0_attn_in['proj_w'], 'L0_attn_proj_b': _L0_attn_in['proj_b'], 'L0_attn_rel_emb': _L0_attn_in['rel_emb'], 'L0_xattn_wq': _L0_xattn_in['wq'], 'L0_xattn_wk': _L0_xattn_in['wk'], 'L0_xattn_wv': _L0_xattn_in['wv'], 'L0_xattn_wo': _L0_xattn_in['wo'], 'L0_ffn_router_w': _L0_ffn_in['router_w'], 'L0_ffn_correction_bias': _L0_ffn_in['correction_bias'], 'L0_ffn_up_w': _L0_ffn_in['up_w'], 'L0_ffn_down_w': _L0_ffn_in['down_w'], 'L0_ffn_shared_up_w': _L0_ffn_in['shared_up_w'], 'L0_ffn_shared_down_w': _L0_ffn_in['shared_down_w']}

def reference(x, ctx_1024, L0_attn_qkv_w, L0_attn_qkv_b, L0_attn_proj_w, L0_attn_proj_b, L0_attn_rel_emb, L0_xattn_wq, L0_xattn_wk, L0_xattn_wv, L0_xattn_wo, L0_ffn_router_w, L0_ffn_correction_bias, L0_ffn_up_w, L0_ffn_down_w, L0_ffn_shared_up_w, L0_ffn_shared_down_w):
    import jax
    import jax.numpy as jnp

    def _L0_attn_ref(x, qkv_w, qkv_b, proj_w, proj_b, rel_emb):
        import jax, jax.numpy as jnp
        import numpy as np
        B, N, D = (1, 256, 128)
        H = 16
        HD = D // H
        MAX_REL = 100
        NUM_EMB = 2 * MAX_REL - 1
        NEG = 100000000.0

        def _rel_pos_logits(q_pos, rel_emb):
            L = q_pos.shape[0]
            pad_len = max(L - MAX_REL, 0)
            start = max(MAX_REL - L, 0)
            padded = jnp.pad(rel_emb, ((0, 0), (pad_len, pad_len), (0, 0)))
            used = padded[:, start:start + 2 * L - 1, :]
            q4 = q_pos.reshape(L, -1, H, HD)
            logits = jnp.einsum('lbhd,hmd->lbhm', q4, used)
            logits = logits.reshape(L, -1, 2 * L - 1)
            if pad_len > 0:
                logits = logits.at[:, :, :pad_len].add(-NEG)
                logits = logits.at[:, :, -pad_len:].add(-NEG)
            bh = logits.shape[1]
            x = jnp.pad(logits, ((0, 0), (0, 0), (0, 1)))
            x = jnp.transpose(x, (1, 0, 2)).reshape(bh, L * 2 * L)
            x = jnp.pad(x, ((0, 0), (0, L - 1)))
            x = x.reshape(bh, L + 1, 2 * L - 1)
            return x[:, :L, L - 1:]
        b, n, d = x.shape
        qkv = x @ qkv_w.T + qkv_b
        qkv = qkv.reshape(b, n, 3, H, HD).transpose(2, 0, 3, 1, 4)
        q, k, v = (qkv[0], qkv[1], qkv[2])
        scale = 1.0 / np.sqrt(HD).astype(np.float32)
        logits = jnp.einsum('bhqd,bhkd->bhqk', q, k) * scale
        q_pos = jnp.transpose(q, (0, 2, 1, 3)).reshape(n, b * H, HD)
        pos = _rel_pos_logits(q_pos, rel_emb).reshape(b, H, n, n)
        probs = jax.nn.softmax(logits + pos, axis=-1)
        out = jnp.einsum('bhqk,bhkd->bhqd', probs, v)
        out = jnp.transpose(out, (0, 2, 1, 3)).reshape(b, n, d)
        return out @ proj_w.T + proj_b

    def _L0_xattn_ref(q, k, v, wq, wk, wv, wo):
        import jax, jax.numpy as jnp
        import numpy as np
        DIM = 128
        N_HEADS = 16
        HEAD_DIM = DIM // N_HEADS
        B, S, _ = q.shape
        H, D = (N_HEADS, HEAD_DIM)
        xq = (q @ wq.T).reshape(B, S, H, D).transpose(0, 2, 1, 3)
        xk = (k @ wk.T).reshape(B, S, H, D).transpose(0, 2, 1, 3)
        xv = (v @ wv.T).reshape(B, S, H, D).transpose(0, 2, 1, 3)
        scores = jnp.einsum('bhqd,bhkd->bhqk', xq, xk) / jnp.sqrt(jnp.float32(D))
        causal = jnp.tril(jnp.ones((S, S), dtype=bool))
        scores = jnp.where(causal, scores, -jnp.inf)
        attn = jax.nn.softmax(scores.astype(jnp.float32), axis=-1).astype(xq.dtype)
        out = jnp.einsum('bhqk,bhkd->bhqd', attn, xv)
        out = out.transpose(0, 2, 1, 3).reshape(B, S, H * D)
        return out @ wo.T

    def _L0_ffn_ref(x, router_w, correction_bias, up_w, down_w, shared_up_w, shared_down_w):
        import jax, jax.numpy as jnp
        import numpy as np
        H = 128
        E = 64
        K = 8
        G = 8
        TOPK_GROUP = 4
        I_MOE = 64
        I_SHARED = 256
        SCALE = 2.5

        def relu2(x):
            return jnp.square(jax.nn.relu(x))

        def _route(xf, router_w, correction_bias):
            T = xf.shape[0]
            logits = xf @ router_w.T
            scores = jax.nn.sigmoid(logits)
            sfc = scores + correction_bias[None, :]
            grp = sfc.reshape(T, G, E // G)
            top2, _ = jax.lax.top_k(grp, 2)
            group_scores = top2.sum(-1)
            _, gidx = jax.lax.top_k(group_scores, TOPK_GROUP)
            gmask = jnp.zeros((T, G), sfc.dtype).at[jnp.arange(T)[:, None], gidx].set(1.0)
            emask = jnp.repeat(gmask, E // G, axis=1)
            masked = jnp.where(emask > 0, sfc, 0.0)
            _, tidx = jax.lax.top_k(masked, K)
            tw = jnp.take_along_axis(scores, tidx, axis=1)
            tw = tw / (tw.sum(-1, keepdims=True) + 1e-20)
            return (tidx, tw * SCALE)
        B, S, Hd = x.shape
        xf = x.reshape(-1, Hd)
        T = xf.shape[0]
        tidx, tw = _route(xf.astype(jnp.float32), router_w, correction_bias)
        combine = jnp.zeros((T, E), xf.dtype).at[jnp.arange(T)[:, None], tidx].add(tw.astype(xf.dtype))

        def body(acc, ew):
            wu, wd, c = ew
            return (acc + c[:, None] * (relu2(xf @ wu) @ wd), None)
        routed, _ = jax.lax.scan(body, jnp.zeros_like(xf), (up_w, down_w, combine.T))
        shared = relu2(xf @ shared_up_w) @ shared_down_w
        return (routed + shared).reshape(B, S, Hd)
    x = _layernorm(x + _L0_attn_ref(x, L0_attn_qkv_w, L0_attn_qkv_b, L0_attn_proj_w, L0_attn_proj_b, L0_attn_rel_emb), axis=-1)
    x = _layernorm(x + _L0_xattn_ref(x, ctx_1024, ctx_1024, L0_xattn_wq, L0_xattn_wk, L0_xattn_wv, L0_xattn_wo), axis=-1)
    x = _layernorm(x + _L0_ffn_ref(x, L0_ffn_router_w, L0_ffn_correction_bias, L0_ffn_up_w, L0_ffn_down_w, L0_ffn_shared_up_w, L0_ffn_shared_down_w), axis=-1)
    return x

_drawn_inputs = setup_inputs


def setup_inputs(seed=0):
    import zlib

    import numpy as np

    out = dict(_drawn_inputs(seed))
    spreads = {'L0_attn_qkv_b': (0.0, 0.317), 'L0_attn_proj_b': (0.0, 0.1)}
    factors = {'L0_attn_qkv_w': 8.0,
     'L0_attn_rel_emb': 8.0,
     'L0_xattn_wq': 8.0,
     'L0_xattn_wk': 8.0,
     'L0_ffn_router_w': 6.981,
     'L0_ffn_correction_bias': 8.0,
     'L0_ffn_up_w': 7.047,
     'L0_ffn_down_w': 6.476,
     'L0_ffn_shared_up_w': 3.175,
     'L0_ffn_shared_down_w': 2.931}
    for name, (base, spread) in spreads.items():
        noise = np.random.default_rng([zlib.crc32(name.encode()), seed]).standard_normal(out[name].shape)
        drawn = base * np.exp(spread * noise) if base else spread * noise
        out[name] = jnp.asarray(drawn.astype(out[name].dtype))
    for name, factor in factors.items():
        out[name] = (out[name] * factor).astype(out[name].dtype)
    return out
```

```python
from contextlib import ExitStack

import concourse.bass as bass
from concourse import mybir

F32 = mybir.dt.float32
BF16 = mybir.dt.bfloat16
F16 = mybir.dt.float16
ALU = mybir.AluOpType
ACT = mybir.ActivationFunctionType
AX = mybir.AxisListType

NB, L, D = 8, 128, 128
H, HD = 16, 8
NG, GH = 4, 4
MAX_REL = 100
NREL = 2 * MAX_REL - 1
REL0 = L - MAX_REL
NEG = 1.0e8
CAUSAL = -1.0e30
SCALE = float(HD) ** -0.5
EPS = 1e-5
E, TOPK, EG, TOPG = 64, 8, 8, 4
ES = E // EG
IM = 64
NPAIR = E // 2
NSH = 2
ROUTE_SCALE = 2.5
LO = 4096.0
HB = 4
HT = HB * L
NV = HD + 1

NU = NB * NG
STAGES = 2 * NU
LT = 1
LV = LT + 1
M = LV + NG + 1
MOE0 = STAGES + LV
CH = NPAIR + NSH
STEPS = MOE0 + 2 * CH + 2
PARTS = 8
BACK, TURN, PROJ, TOKENS, USE = 0, 2, 4, 8, 10
NORM = 7
ROUTE0 = [NG * (NB + HB - 1) + M + USE + 2, NG * (2 * NB - 1) + M + USE + 2]
ROUTE_RATE = [2, 0.5]
CT = [ROUTE0[0] + 5, ROUTE0[1] + 16]

BS, BX, BP, BO, BM, BN = (0, 1), 2, (3, 4), 5, 6, 7
PREP_BANKS = [0, 1, 2, 3, 4, 6, 7]
TASKS = (["w_self", "x0", "q0", "x1", "q1", "rel", "k0", "k1", "v0", "v1", "w_cross", "ctx0", "ctx1"]
         + [f"bias{n}" for n in range(L // 4)]
         + ["kc0", "kc1", "vc0", "vc1", "w_router"])


def by_vector(task):
    if task.startswith("bias"):
        i = 4 * int(task[4:])
        return i < REL0 or i >= MAX_REL
    return task in ("w_self", "rel", "k0", "k1", "v0", "v1")


def out_count(task, vector):
    return sum(by_vector(t) == vector for t in TASKS[:TASKS.index(task) + 1])


def probs_by_vector(U):
    return U < NU and U % 2 == 0


def probs_copied(U):
    v = probs_by_vector(U)
    return v, sum(probs_by_vector(n) == v for n in range(U + 1))


def decoder_layer(nc, x, ctx_in, qkv_w, qkv_b, proj_w, proj_b, rel_emb, wq, wk, wv, wo,
                  router_w, corr, up_w, down_w, sh_up, sh_down, out):
    with ExitStack() as ctx:
        def sb(name, shape, dt=F32):
            return ctx.enter_context(nc.sbuf_tensor(name, shape, dt))

        def sem(name):
            return ctx.enter_context(nc.semaphore(name))

        ps = [ctx.enter_context(nc.psum_tensor(f"bank{n}", [128, 512], F32)) for n in range(8)]

        ident = sb("ident", [128, 128])
        identb = sb("identb", [128, 128], BF16)
        ident_h = sb("ident_h", [128, 128], F16)
        head_mask = sb("head_mask", [128, H])
        slot_mask = sb("slot_mask", [128, GH])
        group_mask = sb("group_mask", [128, NG])
        rel_mask = sb("rel_mask", [128, L])
        causal = sb("causal", [128, L], BF16)
        select = sb("select", [128, NPAIR, 2, IM], F16)
        x_tok = sb("x_tok", [128, NB, D])
        ctx_tok = sb("ctx_tok", [128, NB, D])
        w_raw = sb("w_raw", [128, 4, D])
        wc_raw = sb("wc_raw", [128, 4, D])
        rw_raw = sb("rw_raw", [E, D])
        rel_raw = sb("rel_raw", [128, 2, D])
        qkvb_col = sb("qkvb_col", [128, 3])
        vb_row = sb("vb_row", [128, D])
        pb_row = sb("pb_row", [128, D])
        corr_row = sb("corr_row", [128, E])
        sup = sb("sup", [128, NSH, 128])
        sdn = sb("sdn", [128, NSH, D])
        w_t = sb("w_t", [128, 4, D])
        wc_t = sb("wc_t", [128, 4, D])
        rw_t = sb("rw_t", [128, E])
        rel_t = sb("rel_t", [128, 2 * L])
        x_t = sb("x_t", [128, NB * L])
        q_t = sb("q_t", [128, NB * L])
        k_t = sb("k_t", [128, NB * L])
        ctx_t = sb("ctx_t", [128, NB * L])
        kc_t = sb("kc_t", [128, NB * L])
        v_aug = sb("v_aug", [128, 2, NB, H, NV])
        spread = sb("spread", [128, 2 * 32 * 128])
        q_spread = spread[:, :].rearrange("p (r i n) -> p r i n", r=2, i=32)
        up = spread[:, 0:E * IM].rearrange("p (e i) -> p e i", e=E)
        down = spread[:, E * IM:].rearrange("p (c d) -> p c d", c=NPAIR)
        pos = sb("pos", [128, H * NB, L])
        hidden = pos[:, 0:4 * 9, :].rearrange("p (k r c) i -> p k r (c i)", k=3, r=3)
        relu_sb, cr_sb, act_sb = (hidden[:, n] for n in range(3))
        k_bd = sb("k_bd", [128, 2, GH, L])
        q_bd = sb("q_bd", [128, 2, NG, L])
        qc_t = q_t
        probs = sb("probs", [128, 3, 512])
        probs_t = sb("probs_t", [128, 3, 512])
        neg_max = sb("neg_max", [128, 4, GH])
        o_t = sb("o_t", [128, 2, 512])
        rden = sb("rden", [128, 2, H])
        o_norm = sb("o_norm", [128, 2, D])
        on_t = sb("on_t", [128, 2, D])
        res = sb("res", [128, 2, D])
        stats = sb("stats", [128, 2, 6])
        moments = sb("moments", [128, 2, 2])
        ln_var = sb("ln_var", [128, 2, 1])
        rstd = sb("rstd", [128, 2, 1])
        eps_col = sb("eps_col", [128, 1])
        x1_tok = x2_tok = x_tok
        x1_t = sb("x1_t", [128, 2, L])
        x2_t = x_t
        r_exp = sb("r_exp", [128, HB, E])
        r_one = sb("r_one", [128, HB, E])
        score = sb("score", [128, HB, E])
        biased = sb("biased", [128, HB, E])
        top_in = sb("top_in", [128, HB, EG, 8])
        gscore = sb("gscore", [128, HB, 16])
        gtop = sb("gtop", [128, HB, 8])
        glist = sb("glist", [128, HB, 8])
        grep = sb("grep", [128, HB, 16])
        gkeep = sb("gkeep", [128, HB, EG])
        masked = sb("masked", [128, HB, E])
        etop = sb("etop", [128, HB, 8])
        erep = sb("erep", [128, HB, E])
        chosen = sb("chosen", [128, HB, E])
        weight = sb("weight", [128, HB, E])
        wsum = sb("wsum", [128, HB])
        wsum1 = sb("wsum1", [128, HB])
        wrec = sb("wrec", [128, HB])
        comb = sb("comb", [128, HB, E])
        comb_rest = sb("comb_rest", [128, HB, E])
        comb_split = sb("comb_split", [128, HB, 2, E], F16)
        comb_t = sb("comb_t", [128, NB * L], F16)
        y_t = sb("y_t", [128, HT])
        y_res = sb("y_res", [128, HB, D])
        y_stats = sb("y_stats", [128, HB, 6])
        y_mom = sb("y_mom", [128, HB, 2])
        y_ln = sb("y_ln", [128, HB])
        y_rstd = sb("y_rstd", [128, HB])
        y_out = ctx_tok

        loads = ["x", "w", "w2", "rel", "rel2", "qkvb", "vb", "pb", "ctx", "c0", "c1", "c2", "c3", "rw", "corr",
                 "sup", "sdn", "up", "down"]
        ld = {n: sem(f"ld_{n}") for n in loads}
        ident_made = sem("ident_made")
        masks_made = sem("masks_made")
        consts_made = sem("consts_made")
        pads_made = sem("pads_made")
        xb_made = sem("xb_made")
        pool_chain = sem("pool_chain")
        qk_ready = sem("qk_ready")
        task_done = sem("task_done")
        scores_ready = sem("scores_ready")
        probst_ready = sem("probst_ready")
        pv_done = sem("pv_done")
        back_ready = sem("back_ready")
        ont_ready = sem("ont_ready")
        proj_ready = sem("proj_ready")
        xt_ready = sem("xt_ready")
        q_ready = sem("q_ready")
        logit_ready = sem("logit_ready")
        ct_ready = sem("ct_ready")
        h_ready = sem("h_ready")
        c_ready = sem("c_ready")
        down_done = sem("down_done")
        y_ready = sem("y_ready")
        yback_ready = sem("yback_ready")
        bank_zero = sem("bank_zero")
        out_v = sem("out_v")
        groups_made = sem("groups_made")
        spread_ready = sem("spread_ready")
        v_chain = sem("v_chain")
        max_ready = sem("max_ready")
        pt_out_v = sem("pt_out_v")
        on_ready = sem("on_ready")
        mom_ready = sem("mom_ready")
        x_norm = sem("x_norm")
        exp_read = sem("exp_read")
        comb_ready = sem("comb_ready")
        act_ready = sem("act_ready")
        ymom_ready = sem("ymom_ready")
        y_done = sem("y_done")
        out_a = sem("out_a")
        a_chain = sem("a_chain")
        exp_done = sem("exp_done")
        pt_out_a = sem("pt_out_a")
        ot_out = sem("ot_out")
        ont_out = sem("ont_out")
        rstd_ready = sem("rstd_ready")
        xt_out = sem("xt_out")
        qc_out = sem("qc_out")
        logit_exp = sem("logit_exp")
        ct_out = sem("ct_out")
        relu_ready = sem("relu_ready")
        y_out_t = sem("y_out_t")
        yrstd_ready = sem("yrstd_ready")
        stored = sem("stored")

        block = ctx.enter_context(nc.Block())

        def bank_of(task):
            return ps[PREP_BANKS[TASKS.index(task) % len(PREP_BANKS)]]

        def spread_key(ap, *shape):
            return ap.broadcast_to(list(shape))

        @block.sync
        def _(sp):
            sp.dma_start(x_tok[:, :, :], x.rearrange("b i d -> i b d")).then_inc(ld["x"], 16)
            sp.dma_start(w_raw[:, 0:3, :], qkv_w.rearrange("(c r) d -> r c d", r=128)).then_inc(ld["w"], 16)
            sp.dma_start(w_raw[:, 3, :], proj_w).then_inc(ld["w2"], 16)
            sp.dma_start(qkvb_col[:, :], qkv_b.rearrange("(c r) -> r c", r=128),
                         allow_slow_non_contiguous=True).then_inc(ld["qkvb"], 16)
            rel_v = rel_emb.rearrange("h m d -> m h d")
            sp.dma_start(rel_raw[:, 0, :].rearrange("m (h d) -> m h d", h=H), rel_v[0:128]).then_inc(ld["rel"], 16)
            sp.dma_start(rel_raw[0:NREL - 128, 1, :].rearrange("m (h d) -> m h d", h=H),
                         rel_v[128:NREL]).then_inc(ld["rel2"], 16)
            sp.dma_start(ctx_tok[:, :, :], ctx_in.rearrange("b i d -> i b d")).then_inc(ld["ctx"], 16)
            sp.dma_start(vb_row[:, :], qkv_b[2 * D:3 * D].partition_broadcast(128)).then_inc(ld["vb"], 16)
            for n, w in enumerate((wq, wk, wv, wo)):
                sp.dma_start(wc_raw[:, n, :], w).then_inc(ld[f"c{n}"], 16)
            sp.dma_start(pb_row[:, :], proj_b.partition_broadcast(128)).then_inc(ld["pb"], 16)
            sp.dma_start(rw_raw[:, :], router_w).then_inc(ld["rw"], 16)
            sp.dma_start(corr_row[:, :], corr.partition_broadcast(128)).then_inc(ld["corr"], 16)
            sp.dma_start(sup[:, :, :], sh_up.rearrange("d (c i) -> d c i", c=NSH)).then_inc(ld["sup"], 16)
            sp.dma_start(sdn[:, :, :], sh_down.rearrange("(c i) d -> i c d", c=NSH)).then_inc(ld["sdn"], 16)
            sp.wait_ge(task_done, TASKS.index(f"bias{L // 4 - 1}") + 1)
            sp.dma_start(up, up_w.rearrange("e d i -> d e i")).then_inc(ld["up"], 16)
            sp.dma_start(down, down_w.rearrange("(c e) i d -> (e i) c d", e=2)).then_inc(ld["down"], 16)
            for f in range(2):
                sp.wait_ge(y_done, f + 1)
                sp.dma_start(out[f * HB:(f + 1) * HB].rearrange("b i d -> i b d"),
                             y_out[:, f * HB:(f + 1) * HB, :]).then_inc(stored, 16)
            sp.wait_ge(stored, 32)

        @block.gpsimd
        def _(pool):
            chain = [0]

            def link(ins):
                chain[0] += 1
                ins.then_inc(pool_chain, 1)
                pool.wait_ge(pool_chain, chain[0])

            link(nc.gpsimd.memset(ident[:, :], 0.0))
            link(nc.gpsimd.affine_select(out=ident[:, :], in_=ident[:, :], compare_op=ALU.not_equal, fill=1.0,
                                         base=0, pattern=[[-1, 128]], channel_multiplier=1))
            nc.gpsimd.tensor_copy(identb[:, :], ident[:, :]).then_inc(ident_made, 1)
            nc.gpsimd.tensor_copy(ident_h[:, :], ident[:, :]).then_inc(pads_made, 1)
            link(nc.gpsimd.memset(head_mask[:, :], 1.0))
            link(nc.gpsimd.affine_select(out=head_mask[:, :], in_=head_mask[:, :], compare_op=ALU.is_ge, fill=0.0,
                                         base=0, pattern=[[-HD, H]], channel_multiplier=1))
            nc.gpsimd.affine_select(out=head_mask[:, :], in_=head_mask[:, :], compare_op=ALU.is_ge, fill=0.0,
                                    base=HD - 1, pattern=[[HD, H]], channel_multiplier=-1).then_inc(masks_made, 1)
            nc.gpsimd.memset(rel_t[:, :], 0.0).then_inc(pads_made, 1)
            nc.gpsimd.memset(v_aug[:, :, :, :, HD:NV], 1.0).then_inc(pads_made, 1)
            link(nc.gpsimd.memset(rel_mask[:, :], 0.0))
            link(nc.gpsimd.affine_select(out=rel_mask[:, :], in_=rel_mask[:, :], compare_op=ALU.is_ge, fill=-NEG,
                                         base=MAX_REL - 1, pattern=[[1, L]], channel_multiplier=-1))
            nc.gpsimd.affine_select(out=rel_mask[:, :], in_=rel_mask[:, :], compare_op=ALU.is_ge, fill=-NEG,
                                    base=MAX_REL - 1, pattern=[[-1, L]], channel_multiplier=1).then_inc(masks_made, 1)
            link(nc.gpsimd.memset(causal[:, :], 0.0))
            nc.gpsimd.affine_select(out=causal[:, :], in_=causal[:, :], compare_op=ALU.is_ge, fill=CAUSAL,
                                    base=0, pattern=[[-1, L]], channel_multiplier=1).then_inc(consts_made, 1)
            nc.gpsimd.memset(eps_col[:, :], EPS).then_inc(consts_made, 1)
            nc.gpsimd.memset(gscore[:, :, 8:16], -3.0e38).then_inc(consts_made, 1)
            nc.gpsimd.memset(glist[:, :, TOPG:8], -3.0e38).then_inc(consts_made, 1)
            pool.wait_ge(ld["x"], 16)
            pool.wait_ge(ld["pb"], 16)
            pool.wait_ge(task_done, TASKS.index("x1") + 1)
            nc.gpsimd.tensor_tensor(x_tok[:, :, :], x_tok[:, :, :],
                                    pb_row[:, :].unsqueeze(1).broadcast_to([128, NB, D]), ALU.add).then_inc(xb_made, 1)

            for B in range(2 * NB):
                b, r = B % NB, B % 2
                if B >= 2:
                    pool.wait_ge(scores_ready, 4 * (B - 1))
                if B == 0:
                    pool.wait_ge(groups_made, 2)
                    pool.wait_ge(out_v, out_count("k1", True))
                    pool.wait_ge(out_a, out_count("q1", False))
                if B == NB:
                    pool.wait_ge(out_a, out_count("kc1", False))
                keys = (k_t if B < NB else kc_t)[:, b * L:(b + 1) * L]
                nc.gpsimd.tensor_tensor(k_bd[:, r], keys.unsqueeze(1).broadcast_to([128, GH, L]),
                                        slot_mask[:, :].unsqueeze(2).broadcast_to([128, GH, L]),
                                        ALU.mult).then_inc(qk_ready, 1)
                if B >= NB:
                    pool.wait_ge(qc_out, b + 1)
                queries = (q_t if B < NB else qc_t)[:, b * L:(b + 1) * L]
                nc.gpsimd.tensor_tensor(q_bd[:, r], queries.unsqueeze(1).broadcast_to([128, NG, L]),
                                        group_mask[:, :].unsqueeze(2).broadcast_to([128, NG, L]),
                                        ALU.mult).then_inc(qk_ready, 1)
                if B == 1:
                    link(nc.gpsimd.memset(select[:, :, :, :], 0.0))
                    link(nc.gpsimd.affine_select(out=select[:, :, :, :], in_=select[:, :, :, :],
                                                 compare_op=ALU.not_equal, fill=1.0, base=0,
                                                 pattern=[[-2, NPAIR], [-1, 2], [0, IM]], channel_multiplier=1))
                    nc.gpsimd.affine_select(out=select[:, :, :, :], in_=select[:, :, :, :],
                                            compare_op=ALU.not_equal, fill=1.0 / LO, base=-E,
                                            pattern=[[-2, NPAIR], [-1, 2], [0, IM]],
                                            channel_multiplier=1).then_inc(consts_made, 1)

        @block.tensor
        def _(pe):
            def start(task):
                n = TASKS.index(task)
                if n >= len(PREP_BANKS):
                    before = TASKS[n - len(PREP_BANKS)]
                    v = by_vector(before)
                    pe.wait_ge(out_v if v else out_a, out_count(before, v))

            def transposes(task, blocks, rows=128):
                start(task)
                for n, src in enumerate(blocks):
                    cols = src.shape[0]
                    last = nc.tensor.transpose(bank_of(task)[:, n * 128:n * 128 + cols], src, ident[0:cols, 0:cols])
                last.then_inc(task_done, 1)

            def project(task, w, src, half):
                start(task)
                nc.tensor.matmul(bank_of(task)[:, :], w, src[:, half * HT:(half + 1) * HT],
                                 start=True, stop=True).then_inc(task_done, 1)

            def values(task, w, src, half):
                start(task)
                for n in range(HB):
                    b = half * HB + n
                    last = nc.tensor.matmul(bank_of(task)[:, n * D:(n + 1) * D], src[:, b * L:(b + 1) * L], w,
                                            start=True, stop=True)
                last.then_inc(task_done, 1)

            pe.wait_ge(ident_made, 1)
            pe.wait_ge(ld["w"], 16)
            pe.wait_ge(ld["w2"], 16)
            transposes("w_self", [w_raw[:, n, :] for n in range(4)])
            pe.wait_ge(ld["x"], 16)
            transposes("x0", [x_tok[:, b, :] for b in range(HB)])
            pe.wait_ge(out_v, out_count("w_self", True))
            pe.wait_ge(out_a, out_count("x0", False))
            project("q0", w_t[:, 0, :], x_t, 0)
            transposes("x1", [x_tok[:, b, :] for b in range(HB, NB)])
            pe.wait_ge(out_a, out_count("x1", False))
            project("q1", w_t[:, 0, :], x_t, 1)
            pe.wait_ge(ld["rel"], 16)
            pe.wait_ge(ld["rel2"], 16)
            transposes("rel", [rel_raw[:, 0, :], rel_raw[0:NREL - 128, 1, :]])
            project("k0", w_t[:, 1, :], x_t, 0)
            project("k1", w_t[:, 1, :], x_t, 1)
            values("v0", w_t[:, 2, :], x_t, 0)
            values("v1", w_t[:, 2, :], x_t, 1)
            for n in range(4):
                pe.wait_ge(ld[f"c{n}"], 16)
            transposes("w_cross", [wc_raw[:, n, :] for n in range(4)])
            pe.wait_ge(ld["ctx"], 16)
            transposes("ctx0", [ctx_tok[:, b, :] for b in range(HB)])
            transposes("ctx1", [ctx_tok[:, b, :] for b in range(HB, NB)])
            pe.wait_ge(out_v, out_count("rel", True))
            for n in range(L // 4):
                start(f"bias{n}")
                if n % 8 == 0:
                    pe.wait_ge(spread_ready, n // 8 + 1)
                for m in range(4):
                    i = 4 * n + m
                    last = nc.tensor.matmul(bank_of(f"bias{n}")[:, m * 128:(m + 1) * 128],
                                            rel_t[:, L - 1 - i:2 * L - 1 - i], q_spread[:, i // 32 % 2, i % 32, :],
                                            start=True, stop=True)
                last.then_inc(task_done, 1)
            pe.wait_ge(out_a, out_count("ctx1", False))
            project("kc0", wc_t[:, 1, :], ctx_t, 0)
            project("kc1", wc_t[:, 1, :], ctx_t, 1)
            values("vc0", wc_t[:, 2, :], ctx_t, 0)
            values("vc1", wc_t[:, 2, :], ctx_t, 1)
            pe.wait_ge(ld["rw"], 16)
            transposes("w_router", [rw_raw[:, :]])
            pe.wait_ge(out_v, sum(by_vector(t) for t in TASKS))
            pe.wait_ge(out_a, sum(not by_vector(t) for t in TASKS))
            pe.wait_ge(bank_zero, 1)
            pe.wait_ge(consts_made, 1)
            pe.wait_ge(pads_made, 3)

            def scores(U):
                B, g = U // NG, U % NG
                b, r, bank = B % NB, B % 2, ps[BS[U % 2]]
                if U >= 2:
                    pe.wait_ge(exp_done, U - 1)
                if g == 0:
                    pe.wait_ge(qk_ready, 2 * (B + 1))
                keys = k_bd[:, r].rearrange("p h j -> p (h j)")
                if U < NU:
                    for h4 in range(GH):
                        row = (g * GH + h4) * NB + b
                        nc.tensor.matmul(bank[:, h4 * L:(h4 + 1) * L], pos[:, row, :], ident[:, :],
                                         start=(h4 == 0), stop=False, is_transpose=True, skip_group_check=True)
                    last = nc.tensor.matmul(bank[:, :], q_bd[:, r, g, :], keys, start=False, stop=True,
                                            skip_group_check=True)
                else:
                    nc.tensor.matmul(bank[:, :].rearrange("p (h j) -> p h j", h=GH), identb[:, :],
                                     causal[:, :].unsqueeze(1).broadcast_to([128, GH, L]), start=True, stop=False)
                    last = nc.tensor.matmul(bank[:, :], q_bd[:, r, g, :], keys, start=False, stop=True)
                last.then_inc(scores_ready, 1)

            def wait_probs(U):
                v, n = probs_copied(U)
                pe.wait_ge(pt_out_v if v else pt_out_a, n)

            def transpose_probs(U):
                pe.wait_ge(exp_done, U + 1)
                if U >= 2:
                    wait_probs(U - 2)
                for h4 in range(GH):
                    last = nc.tensor.transpose(ps[BP[U % 2]][:, h4 * L:(h4 + 1) * L],
                                               probs[:, U % 3, h4 * L:(h4 + 1) * L], ident[:, :])
                last.then_inc(probst_ready, 1)

            def values_of(U):
                B, g = U // NG, U % NG
                wait_probs(U)
                if g == 0 and B >= 1:
                    pe.wait_ge(ot_out, B)
                for h4 in range(GH):
                    last = nc.tensor.matmul(ps[BO][32 * h4:32 * h4 + NV, g * L:(g + 1) * L],
                                            v_aug[:, B // NB, B % NB, g * GH + h4, :],
                                            probs_t[:, U % 3, h4 * L:(h4 + 1) * L], start=True, stop=True)
                last.then_inc(pv_done, 1)

            def back(B):
                pe.wait_ge(ot_out, B + 1)
                if B >= 1:
                    pe.wait_ge(on_ready, B)
                for g in range(NG):
                    last = nc.tensor.transpose(ps[BM][:, g * 128:(g + 1) * 128], o_t[:, B % 2, g * 128:(g + 1) * 128],
                                               ident[:, :])
                last.then_inc(back_ready, 1)

            def turn_outputs(B):
                pe.wait_ge(on_ready, B + 1)
                if B >= 2:
                    pe.wait_ge(xt_out, B - 1)
                if NG * B + M + TURN > CT[0]:
                    pe.wait_ge(ct_out, 1)
                nc.tensor.transpose(ps[BN][:, 0:128], o_norm[:, B % 2, :], ident[:, :]).then_inc(ont_ready, 1)

            def read_tokens(B):
                pe.wait_ge(qc_out, B + 1) if B < NB else pe.wait_ge(logit_exp, B - NB + 1)

            def output_projection(B):
                pe.wait_ge(ont_out, B + 1)
                if B >= 1:
                    pe.wait_ge(mom_ready, B)
                if B >= 2:
                    read_tokens(B - 2)
                w = w_t[:, 3, :] if B < NB else wc_t[:, 3, :]
                nc.tensor.matmul(ps[BX][:, 0:D], on_t[:, B % 2, :], w, start=True, stop=True)\
                    .then_inc(proj_ready, 1)

            def turn_tokens(B):
                pe.wait_ge(x_norm, B + 1)
                src = (x1_tok if B < NB else x2_tok)[:, B % NB, :]
                pe.wait_ge(ont_out, min(B + 2, 2 * NB))
                if NG * B + M + TOKENS > CT[0]:
                    pe.wait_ge(ct_out, 1)
                nc.tensor.transpose(ps[BN][:, 0:D], src, ident[:, :]).then_inc(xt_ready, 1)

            def use_tokens(B):
                b = B % NB
                pe.wait_ge(xt_out, B + 1)
                pe.wait_ge(mom_ready, min(B + 2, 2 * NB))
                if B == 2 * NB - 1:
                    read_tokens(B - 1)
                if B < NB:
                    nc.tensor.matmul(ps[BX][:, 0:L], wc_t[:, 0, :], x1_t[:, b % 2, :], start=True, stop=True)\
                        .then_inc(q_ready, 1)
                else:
                    nc.tensor.matmul(ps[BX][:, 0:E], x2_t[:, b * L:(b + 1) * L], rw_t[:, :],
                                     start=True, stop=True).then_inc(logit_ready, 1)

            def turn_weights(f):
                pe.wait_ge(comb_ready, f + 1)
                pe.wait_ge(ont_out, min((CT[f] - M - TURN) // NG + 1, 2 * NB))
                pe.wait_ge(xt_out, min((CT[f] - M - TOKENS) // NG + 1, 2 * NB))
                for n in range(HB):
                    last = nc.tensor.transpose(ps[BN][:, n * 64:(n + 1) * 64].bitcast(F16),
                                               comb_split[:, n, :, :].rearrange("p s e -> p (s e)"), ident_h[:, :])
                last.then_inc(ct_ready, 1)

            def expert_up(k):
                f, c = k // CH, k % CH - NSH
                tokens = x2_t[:, f * HT:(f + 1) * HT]
                if k >= 2:
                    pe.wait_ge(relu_ready, k - 1)
                if c == -NSH:
                    pe.wait_ge(xt_out, NB + (f + 1) * HB)
                if k == 0:
                    pe.wait_ge(ld["up"], 16)
                    pe.wait_ge(ld["sup"], 16)
                    pe.wait_ge(exp_done, STAGES)
                w = up[:, 2 * c:2 * c + 2, :].rearrange("p e i -> p (e i)") if c >= 0 else sup[:, c + NSH, :]
                nc.tensor.matmul(ps[BS[k % 2]][:, :], w, tokens, start=True, stop=True).then_inc(h_ready, 1)
                if c >= 0:
                    n = f * NPAIR + c
                    if n >= 2:
                        pe.wait_ge(act_ready, k - 1 if c >= 2 else k - 1 - NSH)
                    if c == 0:
                        pe.wait_ge(ct_out, f + 1)
                    if n == 0:
                        wait_probs(STAGES - 1)
                        wait_probs(STAGES - 2)
                        pe.wait_ge(consts_made, 5)
                    nc.tensor.matmul(ps[BP[n % 2]][:, :], select[:, c].rearrange("p e i -> p (e i)"),
                                     comb_t[:, f * HT:(f + 1) * HT], start=True, stop=True).then_inc(c_ready, 1)

            def expert_down(k):
                f, c = k // CH, k % CH - NSH
                pe.wait_ge(act_ready, k + 1)
                if k == 0:
                    pe.wait_ge(ld["down"], 16)
                    pe.wait_ge(ld["sdn"], 16)
                    pe.wait_ge(ot_out, 2 * NB)
                if k == CH:
                    pe.wait_ge(ct_out, 2)
                w = down[:, c, :] if c >= 0 else sdn[:, c + NSH, :]
                nc.tensor.matmul(ps[(BO, BN)[f]][:, :], w, act_sb[:, k % 3], start=(c == -NSH),
                                 stop=(c == NPAIR - 1)).then_inc(down_done, 1)

            def turn_y(f):
                pe.wait_ge(y_out_t, f + 1)
                if f == 0:
                    pe.wait_ge(on_ready, 2 * NB)
                else:
                    pe.wait_ge(ymom_ready, 1)
                for n in range(HB):
                    last = nc.tensor.transpose(ps[BM][:, n * D:(n + 1) * D], y_t[:, n * L:(n + 1) * L], ident[:, :])
                last.then_inc(yback_ready, 1)

            for s in range(STEPS):
                k = s - MOE0
                if s < STAGES:
                    scores(s)
                if s in CT:
                    turn_weights(CT.index(s))
                if 0 <= k < 2 * CH:
                    expert_up(k)
                for m, part in ((M + BACK, back), (M + TURN, turn_outputs), (M + PROJ, output_projection),
                                (M + TOKENS, turn_tokens), (M + USE, use_tokens)):
                    if (s - m) % NG == 0 and 0 <= (s - m) // NG < 2 * NB:
                        part((s - m) // NG)
                if 0 <= s - LT < STAGES:
                    transpose_probs(s - LT)
                if 0 <= s - LV < STAGES:
                    values_of(s - LV)
                if k == CH + 3:
                    turn_y(0)
                if 2 <= k:
                    expert_down(k - 2)
            turn_y(1)

        @block.scalar
        def _(act):
            chain = [0]

            def link(ins):
                chain[0] += 1
                ins.then_inc(a_chain, 1)
                act.wait_ge(a_chain, chain[0])

            act.preload_act_table_set("natural_log_exp_and_others")

            def done(task):
                act.wait_ge(task_done, TASKS.index(task) + 1)
                return bank_of(task)[:, :]

            nc.scalar.copy(x_t[:, 0:HT], done("x0")).then_inc(out_a, 1)
            act.wait_ge(ld["qkvb"], 16)
            nc.scalar.activation(q_t[:, 0:HT], done("q0"), ACT.Identity, bias=qkvb_col[:, 0:1]).then_inc(out_a, 1)
            nc.scalar.copy(x_t[:, HT:], done("x1")).then_inc(out_a, 1)
            nc.scalar.activation(q_t[:, HT:], done("q1"), ACT.Identity, bias=qkvb_col[:, 0:1]).then_inc(out_a, 1)
            nc.scalar.copy(wc_t[:, :, :].rearrange("p c d -> p (c d)"), done("w_cross")).then_inc(out_a, 1)
            nc.scalar.copy(ctx_t[:, 0:HT], done("ctx0")).then_inc(out_a, 1)
            nc.scalar.copy(ctx_t[:, HT:], done("ctx1")).then_inc(out_a, 1)
            for n in range(L // 4):
                if not by_vector(f"bias{n}"):
                    nc.scalar.copy(pos[:, :, 4 * n:4 * n + 4],
                                   done(f"bias{n}").rearrange("p (i r) -> p r i", i=4)).then_inc(out_a, 1)
            nc.scalar.mul(kc_t[:, 0:HT], done("kc0"), SCALE).then_inc(out_a, 1)
            nc.scalar.mul(kc_t[:, HT:], done("kc1"), SCALE).then_inc(out_a, 1)
            for f in range(2):
                nc.scalar.copy(v_aug[:, 1, f * HB:(f + 1) * HB, :, 0:HD].rearrange("p b h d -> p (b h) d"),
                               done(f"vc{f}").rearrange("p (n d) -> p n d", d=HD)).then_inc(out_a, 1)
            nc.scalar.copy(rw_t[:, :], done("w_router")[:, 0:E]).then_inc(out_a, 1)
            act.wait_ge(consts_made, 4)

            def exps(U):
                act.wait_ge(max_ready, U + 1)
                if U >= 3:
                    act.wait_ge(probst_ready, U - 2)
                for h4 in range(GH):
                    last = nc.scalar.activation(probs[:, U % 3, h4 * L:(h4 + 1) * L],
                                                ps[BS[U % 2]][:, h4 * L:(h4 + 1) * L], ACT.Exp,
                                                bias=neg_max[:, U % 4, h4:h4 + 1])
                last.then_inc(exp_done, 1)

            def probs_out(U):
                act.wait_ge(probst_ready, U + 1)
                if U >= 3:
                    act.wait_ge(pv_done, U - 2)
                nc.scalar.copy(probs_t[:, U % 3, :], ps[BP[U % 2]][:, :]).then_inc(pt_out_a, 1)

            def outputs_out(B):
                act.wait_ge(pv_done, NG * (B + 1))
                if B >= 2:
                    act.wait_ge(back_ready, B - 1)
                nc.scalar.copy(o_t[:, B % 2, :], ps[BO][:, :]).then_inc(ot_out, 1)

            def turned_out(B):
                act.wait_ge(ont_ready, B + 1)
                if B >= 2:
                    act.wait_ge(proj_ready, B - 1)
                nc.scalar.copy(on_t[:, B % 2, :], ps[BN][:, 0:128]).then_inc(ont_out, 1)

            def deviation(B):
                act.wait_ge(mom_ready, B + 1)
                link(nc.scalar.activation(ln_var[:, B % 2], moments[:, B % 2, 1:2], ACT.Ln, bias=eps_col[:, :]))
                nc.scalar.activation(rstd[:, B % 2], ln_var[:, B % 2], ACT.Exp, scale=-0.5).then_inc(rstd_ready, 1)

            def tokens_out(B):
                act.wait_ge(xt_ready, B + 1)
                b = B % NB
                if 2 <= B < NB:
                    act.wait_ge(q_ready, B - 1)
                if B == NB:
                    act.wait_ge(task_done, len(TASKS))
                dst = x1_t[:, b % 2, :] if B < NB else x2_t[:, b * L:(b + 1) * L]
                nc.scalar.copy(dst, ps[BN][:, 0:D]).then_inc(xt_out, 1)

            def queries_out(B):
                b = B % NB
                if B < NB:
                    act.wait_ge(q_ready, b + 1)
                    act.wait_ge(qk_ready, 2 * (b + 1))
                    nc.scalar.copy(qc_t[:, b * L:(b + 1) * L], ps[BX][:, 0:L]).then_inc(qc_out, 1)
                else:
                    act.wait_ge(logit_ready, b + 1)
                    if b == HB:
                        act.wait_ge(exp_read, 1)
                    nc.scalar.activation(r_exp[:, b % HB, :], ps[BX][:, 0:E], ACT.Exp, scale=-1.0)\
                        .then_inc(logit_exp, 1)

            def weights_out(f):
                act.wait_ge(ct_ready, f + 1)
                nc.scalar.copy(comb_t[:, f * HT:(f + 1) * HT], ps[BN][:, 0:HT // 2].bitcast(F16)).then_inc(ct_out, 1)

            def relu(k):
                act.wait_ge(h_ready, k + 1)
                if k >= 3:
                    act.wait_ge(act_ready, k - 2)
                nc.scalar.activation(relu_sb[:, k % 3], ps[BS[k % 2]][:, :], ACT.Relu).then_inc(relu_ready, 1)

            def y_copy(f):
                act.wait_ge(down_done, (f + 1) * CH)
                if f == 1:
                    act.wait_ge(yback_ready, 1)
                nc.scalar.copy(y_t[:, :], ps[(BO, BN)[f]][:, :]).then_inc(y_out_t, 1)

            def y_deviation(f):
                act.wait_ge(ymom_ready, f + 1)
                link(nc.scalar.activation(y_ln[:, :], y_mom[:, :, 1], ACT.Ln, bias=eps_col[:, :]))
                nc.scalar.activation(y_rstd[:, :], y_ln[:, :], ACT.Exp, scale=-0.5).then_inc(yrstd_ready, 1)

            for s in range(STEPS):
                k = s - MOE0
                for m, part in ((M - 1, outputs_out), (M + TURN + 1, turned_out), (M + TOKENS + 1, tokens_out),
                                (M + USE + 1, queries_out)):
                    if (s - m) % NG == 0 and 0 <= (s - m) // NG < 2 * NB:
                        part((s - m) // NG)
                if s in CT:
                    weights_out(CT.index(s))
                if s < STAGES:
                    exps(s)
                if 0 <= s - LT < STAGES and not probs_by_vector(s - LT):
                    probs_out(s - LT)
                if 0 <= k < 2 * CH:
                    relu(k)
                if (s - M - PROJ - 1) % NG == 0 and 0 <= (s - M - PROJ - 1) // NG < 2 * NB:
                    deviation((s - M - PROJ - 1) // NG)
                if k == CH + 2:
                    y_copy(0)
                if k == CH + 4:
                    y_deviation(0)
            y_copy(1)
            y_deviation(1)

        @block.vector
        def _(dve):
            chain = [0]

            def link(ins):
                chain[0] += 1
                ins.then_inc(v_chain, 1)
                dve.wait_ge(v_chain, chain[0])

            def done(task):
                dve.wait_ge(task_done, TASKS.index(task) + 1)
                return bank_of(task)[:, :]

            nc.vector.memset(ps[BO][:, :], 0.0).then_inc(bank_zero, 1)
            dve.wait_ge(masks_made, 1)
            nc.vector.tensor_reduce(slot_mask[:, :], head_mask[:, :].rearrange("p (g h) -> p h g", g=NG),
                                    AX.X, ALU.add).then_inc(groups_made, 1)
            nc.vector.tensor_reduce(group_mask[:, :], head_mask[:, :].rearrange("p (g h) -> p g h", g=NG),
                                    AX.X, ALU.add).then_inc(groups_made, 1)
            nc.vector.tensor_copy(w_t[:, :, :].rearrange("p c d -> p (c d)"), done("w_self")).then_inc(out_v, 1)
            dve.wait_ge(pads_made, 2)
            nc.vector.tensor_copy(rel_t[:, REL0:REL0 + NREL], done("rel")[:, 0:NREL]).then_inc(out_v, 1)

            def spread_queries(c):
                if c >= 2:
                    dve.wait_ge(task_done, TASKS.index(f"bias{8 * (c - 1) - 1}") + 1)
                src = q_t[:, 32 * NB * c:32 * NB * (c + 1)].rearrange("p (i b) -> p i b", b=NB)
                for h in range(H):
                    last = nc.vector.tensor_scalar(q_spread[:, c % 2, :, h * NB:(h + 1) * NB], src,
                                                   head_mask[:, h:h + 1], None, ALU.mult)
                last.then_inc(spread_ready, 1)

            def keys_out(half):
                nc.vector.tensor_scalar(k_t[:, half * HT:(half + 1) * HT], done(f"k{half}"), qkvb_col[:, 1:2], SCALE,
                                        ALU.add, ALU.mult).then_inc(out_v, 1)

            def values_out(half):
                nc.vector.tensor_tensor(v_aug[:, 0, half * HB:(half + 1) * HB, :, 0:HD],
                                        done(f"v{half}").rearrange("p (b h d) -> p b h d", b=HB, h=H),
                                        vb_row[:, :].rearrange("p (h d) -> p h d", h=H).unsqueeze(1)
                                        .broadcast_to([128, HB, H, HD]), ALU.add).then_inc(out_v, 1)

            def bias_out(n):
                nc.vector.tensor_tensor(pos[:, :, 4 * n:4 * n + 4], done(f"bias{n}").rearrange("p (i r) -> p r i", i=4),
                                        rel_mask[:, 4 * n:4 * n + 4].unsqueeze(1).broadcast_to([128, H * NB, 4]),
                                        ALU.add).then_inc(out_v, 1)

            dve.wait_ge(out_a, out_count("q0", False))
            spread_queries(0)
            dve.wait_ge(ld["qkvb"], 16)
            keys_out(0)
            keys_out(1)
            dve.wait_ge(ld["vb"], 16)
            values_out(0)
            values_out(1)
            spread_queries(1)
            dve.wait_ge(masks_made, 2)
            for n in range(L // 4):
                if n == 7:
                    dve.wait_ge(out_a, out_count("q1", False))
                if n in (7, 16):
                    spread_queries(2 + (n > 8))
                if by_vector(f"bias{n}"):
                    bias_out(n)

            def maxima(U):
                dve.wait_ge(scores_ready, U + 1)
                if U >= 4:
                    dve.wait_ge(exp_done, U - 3)
                nc.vector.tensor_reduce(neg_max[:, U % 4, :], ps[BS[U % 2]][:, :].rearrange("p (h j) -> p h j", h=GH),
                                        AX.X, ALU.max, negate=True).then_inc(max_ready, 1)

            def probs_out(U):
                dve.wait_ge(probst_ready, U + 1)
                if U >= 3:
                    dve.wait_ge(pv_done, U - 2)
                nc.vector.tensor_copy(probs_t[:, U % 3, :], ps[BP[U % 2]][:, :]).then_inc(pt_out_v, 1)

            def normalise(B):
                dve.wait_ge(back_ready, B + 1)
                if B >= 2:
                    dve.wait_ge(ont_ready, B - 1)
                o = ps[BM][:, :].rearrange("p (h c) -> p h c", h=H)
                link(nc.vector.reciprocal(rden[:, B % 2, :], o[:, :, HD]))
                nc.vector.tensor_tensor(o_norm[:, B % 2, :].rearrange("p (h d) -> p h d", h=H), o[:, :, 0:HD],
                                        rden[:, B % 2, :].unsqueeze(2).broadcast_to([128, H, HD]), ALU.mult)\
                    .then_inc(on_ready, 1)

            def residual(B):
                dve.wait_ge(proj_ready, B + 1)
                if B == 0:
                    dve.wait_ge(xb_made, 1)
                base = (x_tok if B < NB else x1_tok)[:, B % NB, :]
                link(nc.vector.tensor_tensor(res[:, B % 2, :], ps[BX][:, 0:D], base, ALU.add))
                link(nc.vector.bn_stats(stats[:, B % 2, :], res[:, B % 2, :]))
                nc.vector.bn_aggr(moments[:, B % 2, :], stats[:, B % 2, :]).then_inc(mom_ready, 1)

            def layer_norm(B):
                dve.wait_ge(rstd_ready, B + 1)
                dst = (x1_tok if B < NB else x2_tok)[:, B % NB, :]
                nc.vector.tensor_scalar(dst, res[:, B % 2, :], moments[:, B % 2, 0:1], rstd[:, B % 2, :],
                                        ALU.subtract, ALU.mult).then_inc(x_norm, 1)

            def route(f, part):
                if part == 0:
                    dve.wait_ge(logit_exp, (f + 1) * HB)
                    dve.wait_ge(ld["corr"], 16)
                    nc.vector.tensor_scalar(r_one[:, :, :], r_exp[:, :, :], 1.0, None, ALU.add).then_inc(exp_read, 1)
                    dve.wait_ge(exp_read, f + 1)
                    link(nc.vector.reciprocal(score[:, :, :], r_one[:, :, :]))
                    link(nc.vector.tensor_tensor(biased[:, :, :], score[:, :, :],
                                                 corr_row[:, :].unsqueeze(1).broadcast_to([128, HB, E]), ALU.add))
                if part in (1, 2):
                    for n in range(2 * (part - 1), 2 * part):
                        for g in range(EG):
                            last = nc.vector.max(top_in[:, n, g, :], biased[:, n, g * ES:(g + 1) * ES])
                    link(last)
                if part == 3:
                    link(nc.vector.tensor_tensor(gscore[:, :, 0:EG], top_in[:, :, :, 0], top_in[:, :, :, 1], ALU.add))
                    for n in range(HB):
                        last = nc.vector.max(gtop[:, n, :], gscore[:, n, 0:EG])
                    link(last)
                    link(nc.vector.tensor_copy(glist[:, :, 0:TOPG], gtop[:, :, 0:TOPG]))
                if part == 4:
                    for n in range(HB):
                        last = nc.vector.match_replace(grep[:, n, :], glist[:, n, :], gscore[:, n, :], 3.0e38)
                    link(last)
                    link(nc.vector.tensor_tensor(gkeep[:, :, :], grep[:, :, 0:EG], gscore[:, :, 0:EG], ALU.not_equal))
                    link(nc.vector.tensor_tensor(
                        masked[:, :, :].rearrange("p n (g e) -> p (n g) e", g=EG),
                        biased[:, :, :].rearrange("p n (g e) -> p (n g) e", g=EG),
                        gkeep[:, :, :].rearrange("p n g -> p (n g)").unsqueeze(2).broadcast_to([128, HB * EG, ES]),
                        ALU.mult))
                if part == 5:
                    for n in range(HB):
                        last = nc.vector.max(etop[:, n, :], masked[:, n, :])
                    link(last)
                    for n in range(HB):
                        last = nc.vector.match_replace(erep[:, n, :], etop[:, n, :], masked[:, n, :], 3.0e38)
                    link(last)
                    link(nc.vector.tensor_tensor(chosen[:, :, :], erep[:, :, :], masked[:, :, :], ALU.not_equal))
                if part == 6:
                    link(nc.vector.tensor_tensor(weight[:, :, :], score[:, :, :], chosen[:, :, :], ALU.mult))
                    link(nc.vector.tensor_reduce(wsum[:, :], weight[:, :, :], AX.X, ALU.add))
                    link(nc.vector.tensor_scalar(wsum1[:, :], wsum[:, :], 1e-20, None, ALU.add))
                    link(nc.vector.reciprocal(wrec[:, :], wsum1[:, :]))
                if part == 7:
                    if f:
                        dve.wait_ge(ct_ready, 1)
                    for n in range(HB):
                        last = nc.vector.tensor_scalar(comb[:, n, :], weight[:, n, :], wrec[:, n:n + 1], ROUTE_SCALE,
                                                       ALU.mult, ALU.mult)
                    link(last)
                    link(nc.vector.tensor_copy(comb_split[:, :, 0, :], comb[:, :, :]))
                    link(nc.vector.tensor_tensor(comb_rest[:, :, :], comb[:, :, :], comb_split[:, :, 0, :],
                                                 ALU.subtract))
                    nc.vector.tensor_scalar(comb_split[:, :, 1, :], comb_rest[:, :, :], LO, None, ALU.mult)\
                        .then_inc(comb_ready, 1)

            def activate(k):
                f, c = k // CH, k % CH - NSH
                dve.wait_ge(relu_ready, k + 1)
                if k >= 3:
                    dve.wait_ge(down_done, k - 2)
                r = relu_sb[:, k % 3]
                if c >= 0:
                    n = f * NPAIR + c
                    dve.wait_ge(c_ready, n + 1)
                    link(nc.vector.tensor_tensor(cr_sb[:, k % 3], ps[BP[n % 2]][:, :], r, ALU.mult))
                    r2 = cr_sb[:, k % 3]
                else:
                    r2 = r
                nc.vector.tensor_tensor(act_sb[:, k % 3], r2, r, ALU.mult).then_inc(act_ready, 1)

            def y_residual(f):
                dve.wait_ge(yback_ready, f + 1)
                if f:
                    dve.wait_ge(yrstd_ready, 1)
                link(nc.vector.tensor_tensor(y_res[:, :, :].rearrange("p n d -> p (n d)"), ps[BM][:, :],
                                             x2_tok[:, f * HB:(f + 1) * HB, :].rearrange("p n d -> p (n d)"), ALU.add))
                for n in range(HB):
                    last = nc.vector.bn_stats(y_stats[:, n, :], y_res[:, n, :])
                link(last)
                for n in range(HB):
                    last = nc.vector.bn_aggr(y_mom[:, n, :], y_stats[:, n, :])
                last.then_inc(ymom_ready, 1)

            def y_norm(f):
                dve.wait_ge(yrstd_ready, f + 1)
                for n in range(HB):
                    last = nc.vector.tensor_scalar(y_out[:, f * HB + n, :], y_res[:, n, :], y_mom[:, n, 0:1],
                                                   y_rstd[:, n:n + 1], ALU.subtract, ALU.mult)
                last.then_inc(y_done, 1)

            for s in range(STEPS):
                k = s - MOE0
                for m, part in ((M + BACK + 1, normalise), (M + PROJ + 1, residual), (M + NORM, layer_norm)):
                    if (s - m) % NG == 0 and 0 <= (s - m) // NG < 2 * NB:
                        part((s - m) // NG)
                if s < STAGES:
                    maxima(s)
                if 0 <= s - LT < STAGES and probs_by_vector(s - LT):
                    probs_out(s - LT)
                for f in range(2):
                    for part in range(PARTS):
                        if s - ROUTE0[f] == int(part / ROUTE_RATE[f]):
                            route(f, part)
                if k == CH + 4:
                    y_residual(0)
                if k == CH + 6:
                    y_norm(0)
                if 0 <= k < 2 * CH:
                    activate(k)
            y_residual(1)
            y_norm(1)


_INS = ["x", "ctx_1024", "L0_attn_qkv_w", "L0_attn_qkv_b", "L0_attn_proj_w", "L0_attn_proj_b", "L0_attn_rel_emb",
        "L0_xattn_wq", "L0_xattn_wk", "L0_xattn_wv", "L0_xattn_wo", "L0_ffn_router_w", "L0_ffn_correction_bias",
        "L0_ffn_up_w", "L0_ffn_down_w", "L0_ffn_shared_up_w", "L0_ffn_shared_down_w"]


def kernel(**inputs):
    import numpy as _np
    import concourse.bacc as _bacc
    from concourse import mybir as _mybir
    from concourse.bass_utils import run_bass_kernel_spmd as _run

    nc = _bacc.Bacc("TRN2", target_bir_lowering=False, num_devices=1)
    arrays, args = {}, []
    for name in _INS:
        a = _np.ascontiguousarray(inputs[name])
        arrays[f"in_{name}"] = a
        args.append(nc.dram_tensor(f"in_{name}", a.shape, _mybir.dt.from_np(a.dtype), kind="ExternalInput").ap())
    args.append(nc.dram_tensor("out_0", (NB, L, D), F32, kind="ExternalOutput").ap())
    decoder_layer(nc, *args)
    r = _run(nc, [arrays], core_ids=[0])
    return r.results[0]["out_0"]
```

```python
from contextlib import ExitStack

import concourse.bass as bass
from concourse import mybir

F32 = mybir.dt.float32
BF16 = mybir.dt.bfloat16
F16 = mybir.dt.float16
F32R = mybir.dt.float32r
ALU = mybir.AluOpType
ACT = mybir.ActivationFunctionType
AX = mybir.AxisListType

NB, L, D = 8, 128, 128
H, HD = 16, 8
NG, GH = 4, 4
MAX_REL = 100
NREL = 2 * MAX_REL - 1
REL0 = L - MAX_REL
NEG = 1.0e8
CAUSAL = -1.0e30
SCALE = float(HD) ** -0.5
EPS = 1e-5
E, TOPK, EG, TOPG = 64, 8, 8, 4
ES = E // EG
IM = 64
NPAIR = E // 2
NSH = 2
ROUTE_SCALE = 2.5
LO = 4096.0
HB = 4
HT = HB * L
NV = HD + 1

NU = NB * NG
STAGES = 2 * NU
LT = 1
LV = LT + 1
M = LV + NG + 1
MOE0 = STAGES + LV
CH = NPAIR + NSH
LD = 4
STEPS = MOE0 + 2 * CH + LD
R = LD + 1
PARTS = 8
BACK, TURN, PROJ, TOKENS, USE = 0, 2, 4, 8, 10
NORM = 7
BATCHES = [(range(0, 2), 1), (range(2, 4), 2), (range(4, 8), 0.5)]
ROUTE0 = [NG * (NB + seqs[-1]) + M + USE + 2 for seqs, _ in BATCHES]
CT = [ROUTE0[1] + 5, ROUTE0[2] + 17]

BS, BX, BP, BO, BM, BN = (0, 1), 2, (3, 4), 5, 6, 7
PREP_BANKS = [0, 1, 2, 3, 4, 6, 7]
TASKS = (["w_self", "x0", "q0", "x1", "q1", "rel", "k0", "k1", "v0", "v1", "w_cross", "ctx0", "ctx1"]
         + [f"bias{n}" for n in range(L // 4)]
         + ["kc0", "kc1", "vc0", "vc1", "w_router"])


def by_vector(task):
    if task.startswith("bias"):
        i = 4 * int(task[4:])
        return i < REL0 or i >= MAX_REL
    return task in ("w_self", "rel", "k0", "k1", "v0", "v1")


def out_count(task, vector):
    return sum(by_vector(t) == vector for t in TASKS[:TASKS.index(task) + 1])


def piece(n):
    size = 2 * E * IM // NB
    return n // (NB // 2), slice(n % (NB // 2) * size, (n % (NB // 2) + 1) * size)


def high_by_vector(k):
    return k % 2 == 0


def rest_by_pool(k):
    return k < CH and k % 3 > 0


def count(which, k, value=True):
    return sum(which(n) == value for n in range(k + 1))


def probs_by_vector(U):
    return U < NU and U % 2 == 0


def probs_copied(U):
    v = probs_by_vector(U)
    return v, sum(probs_by_vector(n) == v for n in range(U + 1))


def decoder_layer(nc, x, ctx_in, qkv_w, qkv_b, proj_w, proj_b, rel_emb, wq, wk, wv, wo,
                  router_w, corr, up_w, down_w, sh_up, sh_down, out):
    with ExitStack() as ctx:
        def sb(name, shape, dt=F32):
            return ctx.enter_context(nc.sbuf_tensor(name, shape, dt))

        def sem(name):
            return ctx.enter_context(nc.semaphore(name))

        ps = [ctx.enter_context(nc.psum_tensor(f"bank{n}", [128, 512], F32)) for n in range(8)]

        with ExitStack() as first:
            def sb1(name, shape, dt=F32):
                return first.enter_context(nc.sbuf_tensor(name, shape, dt))

            pos = sb1("pos", [128, H * NB, L])
            k_t = sb1("k_t", [128, NB * L])
            ctx_t = sb1("ctx_t", [128, NB * L])
            w_raw = sb1("w_raw", [128, 4, D])
            wc_raw = sb1("wc_raw", [128, 4, D])
            spread = sb1("spread", [128, 2 * 32 * 128])
        q_spread = spread[:, :].rearrange("p (r i n) -> p r i n", r=2, i=32)
        experts = spread[:, :].rearrange("p (w n) -> p w n", w=2)
        w_hi = sb("w_hi", [128, 2, E * IM], F32R)
        w_lo = sb("w_lo", [128, 2, E * IM], F32R)
        x2_hi = sb("x2_hi", [128, NB * L], F32R)
        x2_lo = sb("x2_lo", [128, NB * L], F32R)
        sh_hi = sb("sh_hi", [128, 2, NSH * 128], F32R)
        sh_lo = sb("sh_lo", [128, 2, NSH * 128], F32R)
        relu_sb = sb("relu_sb", [128, HT])
        sq = sb("sq", [128, 2, HT])
        unit = sb("unit", [128, 3, HT])
        unit_hi = sb("unit_hi", [128, R, HT], F32R)
        unit_lo = sb("unit_lo", [128, R, HT], F32R)

        ident = sb("ident", [128, 128])
        identb = sb("identb", [128, 128], BF16)
        ident_h = sb("ident_h", [128, 128], F16)
        head_mask = sb("head_mask", [128, H])
        slot_mask = sb("slot_mask", [128, GH])
        group_mask = sb("group_mask", [128, NG])
        rel_mask = sb("rel_mask", [128, L])
        causal = sb("causal", [128, L], BF16)
        select = sb("select", [128, NPAIR, 2, IM], F16)
        x_tok = sb("x_tok", [128, NB, D])
        ctx_tok = sb("ctx_tok", [128, NB, D])
        rw_raw = sb("rw_raw", [E, D])
        rel_raw = sb("rel_raw", [128, 2, D])
        qkvb_col = sb("qkvb_col", [128, 3])
        vb_row = sb("vb_row", [128, D])
        pb_row = sb("pb_row", [128, D])
        corr_row = sb("corr_row", [128, E])
        shared = sb("shared", [128, 2, NSH * 128])
        w_t = sb("w_t", [128, 4, D])
        wc_t = sb("wc_t", [128, 4, D])
        rw_t = sb("rw_t", [128, E])
        rel_t = sb("rel_t", [128, 2 * L])
        x_t = sb("x_t", [128, NB * L])
        q_t = sb("q_t", [128, NB * L])
        kc_t = sb("kc_t", [128, NB * L])
        v_aug = sb("v_aug", [128, 2, NB, H, NV])
        k_bd = sb("k_bd", [128, 2, GH, L])
        q_bd = sb("q_bd", [128, 2, NG, L])
        qc_t = q_t
        probs = sb("probs", [128, 3, 512])
        probs_t = sb("probs_t", [128, 3, 512])
        neg_max = sb("neg_max", [128, 4, GH])
        o_t = sb("o_t", [128, 2, 512])
        rden = sb("rden", [128, 2, H])
        o_norm = sb("o_norm", [128, 2, D])
        on_t = sb("on_t", [128, 2, D])
        res = sb("res", [128, 2, D])
        stats = sb("stats", [128, 2, 6])
        moments = sb("moments", [128, 2, 2])
        ln_var = sb("ln_var", [128, 2, 1])
        rstd = sb("rstd", [128, 2, 1])
        eps_col = sb("eps_col", [128, 1])
        x1_tok = x2_tok = x_tok
        x1_t = sb("x1_t", [128, 2, L])
        x2_t = x_t
        r_exp = sb("r_exp", [128, HB, E])
        r_one = sb("r_one", [128, HB, E])
        score = sb("score", [128, HB, E])
        biased = sb("biased", [128, HB, E])
        top_in = sb("top_in", [128, HB, EG, 8])
        gscore = sb("gscore", [128, HB, 16])
        gtop = sb("gtop", [128, HB, 8])
        glist = sb("glist", [128, HB, 8])
        grep = sb("grep", [128, HB, 16])
        gkeep = sb("gkeep", [128, HB, EG])
        masked = sb("masked", [128, HB, E])
        etop = sb("etop", [128, HB, 8])
        erep = sb("erep", [128, HB, E])
        chosen = sb("chosen", [128, HB, E])
        weight = sb("weight", [128, HB, E])
        wsum = sb("wsum", [128, HB])
        wsum1 = sb("wsum1", [128, HB])
        wrec = sb("wrec", [128, HB])
        comb = sb("comb", [128, HB, E])
        comb_rest = sb("comb_rest", [128, HB, E])
        comb_split = sb("comb_split", [128, HB, 2, E], F16)
        comb_t = sb("comb_t", [128, NB * L], F16)
        y_t = sb("y_t", [128, HT])
        y_res = sb("y_res", [128, HB, D])
        y_stats = sb("y_stats", [128, HB, 6])
        y_mom = sb("y_mom", [128, HB, 2])
        y_ln = sb("y_ln", [128, HB])
        y_rstd = sb("y_rstd", [128, HB])
        y_out = ctx_tok

        loads = ["x", "w", "w2", "rel", "rel2", "qkvb", "vb", "pb", "ctx", "c0", "c1", "c2", "c3", "rw", "corr",
                 "sup", "sdn", "up", "down"]
        ld = {n: sem(f"ld_{n}") for n in loads}
        ident_made = sem("ident_made")
        masks_made = sem("masks_made")
        consts_made = sem("consts_made")
        pads_made = sem("pads_made")
        xb_made = sem("xb_made")
        pool_chain = sem("pool_chain")
        w_high = sem("w_high")
        lo_ready_p = sem("lo_ready_p")
        qk_ready = sem("qk_ready")
        task_done = sem("task_done")
        scores_ready = sem("scores_ready")
        probst_ready = sem("probst_ready")
        pv_done = sem("pv_done")
        back_ready = sem("back_ready")
        ont_ready = sem("ont_ready")
        proj_ready = sem("proj_ready")
        xt_ready = sem("xt_ready")
        q_ready = sem("q_ready")
        logit_ready = sem("logit_ready")
        ct_ready = sem("ct_ready")
        h_ready = sem("h_ready")
        c_ready = sem("c_ready")
        down_done = sem("down_done")
        y_ready = sem("y_ready")
        yback_ready = sem("yback_ready")
        bank_zero = sem("bank_zero")
        out_v = sem("out_v")
        groups_made = sem("groups_made")
        spread_ready = sem("spread_ready")
        v_chain = sem("v_chain")
        max_ready = sem("max_ready")
        pt_out_v = sem("pt_out_v")
        on_ready = sem("on_ready")
        mom_ready = sem("mom_ready")
        x_norm = sem("x_norm")
        exp_read = sem("exp_read")
        comb_ready = sem("comb_ready")
        unit_ready = sem("unit_ready")
        hi_ready_v = sem("hi_ready_v")
        lo_ready_v = sem("lo_ready_v")
        w_split = sem("w_split")
        x2_split = sem("x2_split")
        ymom_ready = sem("ymom_ready")
        y_done = sem("y_done")
        out_a = sem("out_a")
        a_chain = sem("a_chain")
        exp_done = sem("exp_done")
        pt_out_a = sem("pt_out_a")
        ot_out = sem("ot_out")
        ont_out = sem("ont_out")
        rstd_ready = sem("rstd_ready")
        xt_out = sem("xt_out")
        qc_out = sem("qc_out")
        logit_exp = sem("logit_exp")
        ct_out = sem("ct_out")
        relu_ready = sem("relu_ready")
        sq_ready = sem("sq_ready")
        hi_ready_a = sem("hi_ready_a")
        y_out_t = sem("y_out_t")
        yrstd_ready = sem("yrstd_ready")
        stored = sem("stored")

        block = ctx.enter_context(nc.Block())

        def bank_of(task):
            return ps[PREP_BANKS[TASKS.index(task) % len(PREP_BANKS)]]

        def wait_high(eng, k):
            v = high_by_vector(k)
            eng.wait_ge(hi_ready_v if v else hi_ready_a, count(high_by_vector, k, v))

        def wait_rest(eng, k):
            p = rest_by_pool(k)
            eng.wait_ge(lo_ready_p if p else lo_ready_v, count(rest_by_pool, k, p))

        @block.sync
        def _(sp):
            sp.dma_start(x_tok[:, :, :], x.rearrange("b i d -> i b d")).then_inc(ld["x"], 16)
            sp.dma_start(w_raw[:, 0:3, :], qkv_w.rearrange("(c r) d -> r c d", r=128)).then_inc(ld["w"], 16)
            sp.dma_start(w_raw[:, 3, :], proj_w).then_inc(ld["w2"], 16)
            sp.dma_start(qkvb_col[:, :], qkv_b.rearrange("(c r) -> r c", r=128),
                         allow_slow_non_contiguous=True).then_inc(ld["qkvb"], 16)
            rel_v = rel_emb.rearrange("h m d -> m h d")
            sp.dma_start(rel_raw[:, 0, :].rearrange("m (h d) -> m h d", h=H), rel_v[0:128]).then_inc(ld["rel"], 16)
            sp.dma_start(rel_raw[0:NREL - 128, 1, :].rearrange("m (h d) -> m h d", h=H),
                         rel_v[128:NREL]).then_inc(ld["rel2"], 16)
            sp.dma_start(ctx_tok[:, :, :], ctx_in.rearrange("b i d -> i b d")).then_inc(ld["ctx"], 16)
            sp.dma_start(vb_row[:, :], qkv_b[2 * D:3 * D].partition_broadcast(128)).then_inc(ld["vb"], 16)
            for n, w in enumerate((wq, wk, wv, wo)):
                sp.dma_start(wc_raw[:, n, :], w).then_inc(ld[f"c{n}"], 16)
            sp.dma_start(pb_row[:, :], proj_b.partition_broadcast(128)).then_inc(ld["pb"], 16)
            sp.dma_start(rw_raw[:, :], router_w).then_inc(ld["rw"], 16)
            sp.dma_start(corr_row[:, :], corr.partition_broadcast(128)).then_inc(ld["corr"], 16)
            sp.dma_start(shared[:, 0, :], sh_up).then_inc(ld["sup"], 16)
            sp.dma_start(shared[:, 1, :].rearrange("p (c d) -> p c d", c=NSH), sh_down.rearrange("(c i) d -> i c d", c=NSH)).then_inc(ld["sdn"], 16)
            sp.wait_ge(task_done, TASKS.index(f"bias{L // 4 - 1}") + 1)
            sp.dma_start(experts[:, 0, :].rearrange("p (e i) -> p e i", e=E), up_w.rearrange("e d i -> d e i")).then_inc(ld["up"], 16)
            sp.dma_start(experts[:, 1, :].rearrange("p (c d) -> p c d", c=NPAIR), down_w.rearrange("(c e) i d -> (e i) c d", e=2)).then_inc(ld["down"], 16)
            for f in range(2):
                sp.wait_ge(y_done, f + 1)
                sp.dma_start(out[f * HB:(f + 1) * HB].rearrange("b i d -> i b d"),
                             y_out[:, f * HB:(f + 1) * HB, :]).then_inc(stored, 16)
            sp.wait_ge(stored, 32)

        @block.gpsimd
        def _(pool):
            chain = [0]

            def link(ins):
                chain[0] += 1
                ins.then_inc(pool_chain, 1)
                pool.wait_ge(pool_chain, chain[0])

            link(nc.gpsimd.memset(ident[:, :], 0.0))
            link(nc.gpsimd.affine_select(out=ident[:, :], in_=ident[:, :], compare_op=ALU.not_equal, fill=1.0,
                                         base=0, pattern=[[-1, 128]], channel_multiplier=1))
            nc.gpsimd.tensor_copy(identb[:, :], ident[:, :]).then_inc(ident_made, 1)
            nc.gpsimd.tensor_copy(ident_h[:, :], ident[:, :]).then_inc(pads_made, 1)
            link(nc.gpsimd.memset(head_mask[:, :], 1.0))
            link(nc.gpsimd.affine_select(out=head_mask[:, :], in_=head_mask[:, :], compare_op=ALU.is_ge, fill=0.0,
                                         base=0, pattern=[[-HD, H]], channel_multiplier=1))
            nc.gpsimd.affine_select(out=head_mask[:, :], in_=head_mask[:, :], compare_op=ALU.is_ge, fill=0.0,
                                    base=HD - 1, pattern=[[HD, H]], channel_multiplier=-1).then_inc(masks_made, 1)
            nc.gpsimd.memset(rel_t[:, :], 0.0).then_inc(pads_made, 1)
            nc.gpsimd.memset(v_aug[:, :, :, :, HD:NV], 1.0).then_inc(pads_made, 1)
            link(nc.gpsimd.memset(rel_mask[:, :], 0.0))
            link(nc.gpsimd.affine_select(out=rel_mask[:, :], in_=rel_mask[:, :], compare_op=ALU.is_ge, fill=-NEG,
                                         base=MAX_REL - 1, pattern=[[1, L]], channel_multiplier=-1))
            nc.gpsimd.affine_select(out=rel_mask[:, :], in_=rel_mask[:, :], compare_op=ALU.is_ge, fill=-NEG,
                                    base=MAX_REL - 1, pattern=[[-1, L]], channel_multiplier=1).then_inc(masks_made, 1)
            link(nc.gpsimd.memset(causal[:, :], 0.0))
            nc.gpsimd.affine_select(out=causal[:, :], in_=causal[:, :], compare_op=ALU.is_ge, fill=CAUSAL,
                                    base=0, pattern=[[-1, L]], channel_multiplier=1).then_inc(consts_made, 1)
            nc.gpsimd.memset(eps_col[:, :], EPS).then_inc(consts_made, 1)
            nc.gpsimd.memset(gscore[:, :, 8:16], -3.0e38).then_inc(consts_made, 1)
            nc.gpsimd.memset(glist[:, :, TOPG:8], -3.0e38).then_inc(consts_made, 1)
            pool.wait_ge(ld["x"], 16)
            pool.wait_ge(ld["pb"], 16)
            pool.wait_ge(task_done, TASKS.index("x1") + 1)
            nc.gpsimd.tensor_tensor(x_tok[:, :, :], x_tok[:, :, :],
                                    pb_row[:, :].unsqueeze(1).broadcast_to([128, NB, D]), ALU.add).then_inc(xb_made, 1)

            for B in range(2 * NB):
                b, r = B % NB, B % 2
                if B >= 2:
                    pool.wait_ge(scores_ready, 4 * (B - 1))
                if B == 0:
                    pool.wait_ge(groups_made, 2)
                    pool.wait_ge(out_v, out_count("k1", True))
                    pool.wait_ge(out_a, out_count("q1", False))
                if B == NB:
                    pool.wait_ge(out_a, out_count("kc1", False))
                keys = (k_t if B < NB else kc_t)[:, b * L:(b + 1) * L]
                nc.gpsimd.tensor_tensor(k_bd[:, r], keys.unsqueeze(1).broadcast_to([128, GH, L]),
                                        slot_mask[:, :].unsqueeze(2).broadcast_to([128, GH, L]),
                                        ALU.mult).then_inc(qk_ready, 1)
                if B >= NB:
                    pool.wait_ge(qc_out, b + 1)
                queries = (q_t if B < NB else qc_t)[:, b * L:(b + 1) * L]
                nc.gpsimd.tensor_tensor(q_bd[:, r], queries.unsqueeze(1).broadcast_to([128, NG, L]),
                                        group_mask[:, :].unsqueeze(2).broadcast_to([128, NG, L]),
                                        ALU.mult).then_inc(qk_ready, 1)
                if B >= NB:
                    if b == 0:
                        pool.wait_ge(scores_ready, NU)
                        pool.wait_ge(ld["sup"], 16)
                        pool.wait_ge(ld["sdn"], 16)
                        pool.wait_ge(ld["up"], 16)
                        nc.gpsimd.tensor_copy(sh_hi[:, :, :], shared[:, :, :])
                    if b == NB // 2:
                        pool.wait_ge(ld["down"], 16)
                    way, cols = piece(b)
                    nc.gpsimd.tensor_copy(w_hi[:, way, cols], experts[:, way, cols]).then_inc(w_high, 1)
                if B == 1:
                    link(nc.gpsimd.memset(select[:, :, :, :], 0.0))
                    link(nc.gpsimd.affine_select(out=select[:, :, :, :], in_=select[:, :, :, :],
                                                 compare_op=ALU.not_equal, fill=1.0, base=0,
                                                 pattern=[[-2, NPAIR], [-1, 2], [0, IM]], channel_multiplier=1))
                    nc.gpsimd.affine_select(out=select[:, :, :, :], in_=select[:, :, :, :],
                                            compare_op=ALU.not_equal, fill=1.0 / LO, base=-E,
                                            pattern=[[-2, NPAIR], [-1, 2], [0, IM]],
                                            channel_multiplier=1).then_inc(consts_made, 1)

            for k in range(2 * CH):
                if rest_by_pool(k):
                    wait_high(pool, k)
                    if k >= R:
                        pool.wait_ge(down_done, k - R + 1)
                    nc.gpsimd.tensor_tensor(unit_lo[:, k % R], unit[:, k % 3], unit_hi[:, k % R],
                                            ALU.subtract).then_inc(lo_ready_p, 1)

        @block.tensor
        def _(pe):
            def start(task):
                n = TASKS.index(task)
                if n >= len(PREP_BANKS):
                    before = TASKS[n - len(PREP_BANKS)]
                    v = by_vector(before)
                    pe.wait_ge(out_v if v else out_a, out_count(before, v))

            def transposes(task, blocks, rows=128):
                start(task)
                for n, src in enumerate(blocks):
                    cols = src.shape[0]
                    last = nc.tensor.transpose(bank_of(task)[:, n * 128:n * 128 + cols], src, ident[0:cols, 0:cols])
                last.then_inc(task_done, 1)

            def project(task, w, src, half):
                start(task)
                nc.tensor.matmul(bank_of(task)[:, :], w, src[:, half * HT:(half + 1) * HT],
                                 start=True, stop=True).then_inc(task_done, 1)

            def values(task, w, src, half):
                start(task)
                for n in range(HB):
                    b = half * HB + n
                    last = nc.tensor.matmul(bank_of(task)[:, n * D:(n + 1) * D], src[:, b * L:(b + 1) * L], w,
                                            start=True, stop=True)
                last.then_inc(task_done, 1)

            pe.wait_ge(ident_made, 1)
            pe.wait_ge(ld["w"], 16)
            pe.wait_ge(ld["w2"], 16)
            transposes("w_self", [w_raw[:, n, :] for n in range(4)])
            pe.wait_ge(ld["x"], 16)
            transposes("x0", [x_tok[:, b, :] for b in range(HB)])
            pe.wait_ge(out_v, out_count("w_self", True))
            pe.wait_ge(out_a, out_count("x0", False))
            project("q0", w_t[:, 0, :], x_t, 0)
            transposes("x1", [x_tok[:, b, :] for b in range(HB, NB)])
            pe.wait_ge(out_a, out_count("x1", False))
            project("q1", w_t[:, 0, :], x_t, 1)
            pe.wait_ge(ld["rel"], 16)
            pe.wait_ge(ld["rel2"], 16)
            transposes("rel", [rel_raw[:, 0, :], rel_raw[0:NREL - 128, 1, :]])
            project("k0", w_t[:, 1, :], x_t, 0)
            project("k1", w_t[:, 1, :], x_t, 1)
            values("v0", w_t[:, 2, :], x_t, 0)
            values("v1", w_t[:, 2, :], x_t, 1)
            for n in range(4):
                pe.wait_ge(ld[f"c{n}"], 16)
            transposes("w_cross", [wc_raw[:, n, :] for n in range(4)])
            pe.wait_ge(ld["ctx"], 16)
            transposes("ctx0", [ctx_tok[:, b, :] for b in range(HB)])
            transposes("ctx1", [ctx_tok[:, b, :] for b in range(HB, NB)])
            pe.wait_ge(out_v, out_count("rel", True))
            for n in range(L // 4):
                start(f"bias{n}")
                if n % 8 == 0:
                    pe.wait_ge(spread_ready, n // 8 + 1)
                for m in range(4):
                    i = 4 * n + m
                    last = nc.tensor.matmul(bank_of(f"bias{n}")[:, m * 128:(m + 1) * 128],
                                            rel_t[:, L - 1 - i:2 * L - 1 - i], q_spread[:, i // 32 % 2, i % 32, :],
                                            start=True, stop=True)
                last.then_inc(task_done, 1)
            pe.wait_ge(out_a, out_count("ctx1", False))
            project("kc0", wc_t[:, 1, :], ctx_t, 0)
            project("kc1", wc_t[:, 1, :], ctx_t, 1)
            values("vc0", wc_t[:, 2, :], ctx_t, 0)
            values("vc1", wc_t[:, 2, :], ctx_t, 1)
            pe.wait_ge(ld["rw"], 16)
            transposes("w_router", [rw_raw[:, :]])
            pe.wait_ge(out_v, sum(by_vector(t) for t in TASKS))
            pe.wait_ge(out_a, sum(not by_vector(t) for t in TASKS))
            pe.wait_ge(bank_zero, 1)
            pe.wait_ge(consts_made, 1)
            pe.wait_ge(pads_made, 3)

            def scores(U):
                B, g = U // NG, U % NG
                b, r, bank = B % NB, B % 2, ps[BS[U % 2]]
                if U >= 2:
                    pe.wait_ge(exp_done, U - 1)
                if g == 0:
                    pe.wait_ge(qk_ready, 2 * (B + 1))
                keys = k_bd[:, r].rearrange("p h j -> p (h j)")
                if U < NU:
                    for h4 in range(GH):
                        row = (g * GH + h4) * NB + b
                        nc.tensor.matmul(bank[:, h4 * L:(h4 + 1) * L], pos[:, row, :], ident[:, :],
                                         start=(h4 == 0), stop=False, is_transpose=True, skip_group_check=True)
                    last = nc.tensor.matmul(bank[:, :], q_bd[:, r, g, :], keys, start=False, stop=True,
                                            skip_group_check=True)
                else:
                    nc.tensor.matmul(bank[:, :].rearrange("p (h j) -> p h j", h=GH), identb[:, :],
                                     causal[:, :].unsqueeze(1).broadcast_to([128, GH, L]), start=True, stop=False)
                    last = nc.tensor.matmul(bank[:, :], q_bd[:, r, g, :], keys, start=False, stop=True)
                last.then_inc(scores_ready, 1)

            def wait_probs(U):
                v, n = probs_copied(U)
                pe.wait_ge(pt_out_v if v else pt_out_a, n)

            def transpose_probs(U):
                pe.wait_ge(exp_done, U + 1)
                if U >= 2:
                    wait_probs(U - 2)
                for h4 in range(GH):
                    last = nc.tensor.transpose(ps[BP[U % 2]][:, h4 * L:(h4 + 1) * L],
                                               probs[:, U % 3, h4 * L:(h4 + 1) * L], ident[:, :])
                last.then_inc(probst_ready, 1)

            def values_of(U):
                B, g = U // NG, U % NG
                wait_probs(U)
                if g == 0 and B >= 1:
                    pe.wait_ge(ot_out, B)
                for h4 in range(GH):
                    last = nc.tensor.matmul(ps[BO][32 * h4:32 * h4 + NV, g * L:(g + 1) * L],
                                            v_aug[:, B // NB, B % NB, g * GH + h4, :],
                                            probs_t[:, U % 3, h4 * L:(h4 + 1) * L], start=True, stop=True)
                last.then_inc(pv_done, 1)

            def back(B):
                pe.wait_ge(ot_out, B + 1)
                if B >= 1:
                    pe.wait_ge(on_ready, B)
                for g in range(NG):
                    last = nc.tensor.transpose(ps[BM][:, g * 128:(g + 1) * 128], o_t[:, B % 2, g * 128:(g + 1) * 128],
                                               ident[:, :])
                last.then_inc(back_ready, 1)

            def turn_outputs(B):
                pe.wait_ge(on_ready, B + 1)
                if B >= 2:
                    pe.wait_ge(xt_out, B - 1)
                if NG * B + M + TURN > CT[0]:
                    pe.wait_ge(ct_out, 1)
                nc.tensor.transpose(ps[BN][:, 0:128], o_norm[:, B % 2, :], ident[:, :]).then_inc(ont_ready, 1)

            def read_tokens(B):
                pe.wait_ge(qc_out, B + 1) if B < NB else pe.wait_ge(logit_exp, B - NB + 1)

            def output_projection(B):
                pe.wait_ge(ont_out, B + 1)
                if B >= 1:
                    pe.wait_ge(mom_ready, B)
                if B >= 2:
                    read_tokens(B - 2)
                w = w_t[:, 3, :] if B < NB else wc_t[:, 3, :]
                nc.tensor.matmul(ps[BX][:, 0:D], on_t[:, B % 2, :], w, start=True, stop=True)\
                    .then_inc(proj_ready, 1)

            def turn_tokens(B):
                pe.wait_ge(x_norm, B + 1)
                src = (x1_tok if B < NB else x2_tok)[:, B % NB, :]
                pe.wait_ge(ont_out, min(B + 2, 2 * NB))
                if NG * B + M + TOKENS > CT[0]:
                    pe.wait_ge(ct_out, 1)
                nc.tensor.transpose(ps[BN][:, 0:D], src, ident[:, :]).then_inc(xt_ready, 1)

            def use_tokens(B):
                b = B % NB
                pe.wait_ge(xt_out, B + 1)
                pe.wait_ge(mom_ready, min(B + 2, 2 * NB))
                if B == 2 * NB - 1:
                    read_tokens(B - 1)
                if B < NB:
                    nc.tensor.matmul(ps[BX][:, 0:L], wc_t[:, 0, :], x1_t[:, b % 2, :], start=True, stop=True)\
                        .then_inc(q_ready, 1)
                else:
                    nc.tensor.matmul(ps[BX][:, 0:E], x2_t[:, b * L:(b + 1) * L], rw_t[:, :],
                                     start=True, stop=True).then_inc(logit_ready, 1)

            def turn_weights(f):
                pe.wait_ge(comb_ready, f + 2)
                pe.wait_ge(ont_out, min((CT[f] - M - TURN) // NG + 1, 2 * NB))
                pe.wait_ge(xt_out, min((CT[f] - M - TOKENS) // NG + 1, 2 * NB))
                for n in range(HB):
                    last = nc.tensor.transpose(ps[BN][:, n * 64:(n + 1) * 64].bitcast(F16),
                                               comb_split[:, n, :, :].rearrange("p s e -> p (s e)"), ident_h[:, :])
                last.then_inc(ct_ready, 1)

            def product(bank, w, act, first, last):
                for n, (a, b) in enumerate(((0, 0), (1, 0), (0, 1))):
                    ins = nc.tensor.matmul(bank, w[a], act[b], start=(first and n == 0), stop=(last and n == 2))
                return ins

            def expert_up(k):
                f, c = k // CH, k % CH - NSH
                if k >= 2:
                    pe.wait_ge(relu_ready, k - 1)
                if c == -NSH:
                    pe.wait_ge(x2_split, (f + 1) * HB)
                if k == 0:
                    pe.wait_ge(w_split, NB)
                    pe.wait_ge(exp_done, STAGES)
                if c >= 0:
                    w = [t[:, 0, c * 128:(c + 1) * 128] for t in (w_hi, w_lo)]
                else:
                    w = [t[:, 0, (c + NSH) * 128:(c + NSH + 1) * 128] for t in (sh_hi, sh_lo)]
                product(ps[BS[k % 2]][:, :], w, [t[:, f * HT:(f + 1) * HT] for t in (x2_hi, x2_lo)],
                        True, True).then_inc(h_ready, 1)

            def spread_weights(k):
                f, c = k // CH, k % CH - NSH
                if c >= 0:
                    n = f * NPAIR + c
                    if n >= 2:
                        pe.wait_ge(unit_ready, k - 1 if c >= 2 else k - 1 - NSH)
                    if c == 0:
                        pe.wait_ge(ct_out, f + 1)
                    if n == 0:
                        wait_probs(STAGES - 1)
                        wait_probs(STAGES - 2)
                        pe.wait_ge(consts_made, 5)
                    nc.tensor.matmul(ps[BP[n % 2]][:, :], select[:, c].rearrange("p e i -> p (e i)"),
                                     comb_t[:, f * HT:(f + 1) * HT], start=True, stop=True).then_inc(c_ready, 1)

            def expert_down(k):
                f, c = k // CH, k % CH - NSH
                wait_rest(pe, k)
                if k == 0:
                    pe.wait_ge(ot_out, 2 * NB)
                if k == CH:
                    pe.wait_ge(ct_out, 2)
                if c >= 0:
                    w = [t[:, 1, c * 128:(c + 1) * 128] for t in (w_hi, w_lo)]
                else:
                    w = [t[:, 1, (c + NSH) * 128:(c + NSH + 1) * 128] for t in (sh_hi, sh_lo)]
                product(ps[(BO, BN)[f]][:, :], w, (unit_hi[:, k % R], unit_lo[:, k % R]), c == -NSH,
                        c == NPAIR - 1).then_inc(down_done, 1)

            def turn_y(f):
                pe.wait_ge(y_out_t, f + 1)
                if f == 0:
                    pe.wait_ge(on_ready, 2 * NB)
                else:
                    pe.wait_ge(ymom_ready, 1)
                for n in range(HB):
                    last = nc.tensor.transpose(ps[BM][:, n * D:(n + 1) * D], y_t[:, n * L:(n + 1) * L], ident[:, :])
                last.then_inc(yback_ready, 1)

            for s in range(STEPS):
                k = s - MOE0
                if s < STAGES:
                    scores(s)
                if s in CT:
                    turn_weights(CT.index(s))
                if 0 <= k < 2 * CH:
                    expert_up(k)
                    spread_weights(k)
                for m, part in ((M + BACK, back), (M + TURN, turn_outputs), (M + PROJ, output_projection),
                                (M + TOKENS, turn_tokens), (M + USE, use_tokens)):
                    if (s - m) % NG == 0 and 0 <= (s - m) // NG < 2 * NB:
                        part((s - m) // NG)
                if 0 <= s - LT < STAGES:
                    transpose_probs(s - LT)
                if 0 <= s - LV < STAGES:
                    values_of(s - LV)
                if k == CH + LD + 2:
                    turn_y(0)
                if LD <= k:
                    expert_down(k - LD)
            turn_y(1)

        @block.scalar
        def _(act):
            chain = [0]

            def link(ins):
                chain[0] += 1
                ins.then_inc(a_chain, 1)
                act.wait_ge(a_chain, chain[0])

            act.preload_act_table_set("natural_log_exp_and_others")

            def done(task):
                act.wait_ge(task_done, TASKS.index(task) + 1)
                return bank_of(task)[:, :]

            nc.scalar.copy(x_t[:, 0:HT], done("x0")).then_inc(out_a, 1)
            act.wait_ge(ld["qkvb"], 16)
            nc.scalar.activation(q_t[:, 0:HT], done("q0"), ACT.Identity, bias=qkvb_col[:, 0:1]).then_inc(out_a, 1)
            nc.scalar.copy(x_t[:, HT:], done("x1")).then_inc(out_a, 1)
            nc.scalar.activation(q_t[:, HT:], done("q1"), ACT.Identity, bias=qkvb_col[:, 0:1]).then_inc(out_a, 1)
            nc.scalar.copy(wc_t[:, :, :].rearrange("p c d -> p (c d)"), done("w_cross")).then_inc(out_a, 1)
            nc.scalar.copy(ctx_t[:, 0:HT], done("ctx0")).then_inc(out_a, 1)
            nc.scalar.copy(ctx_t[:, HT:], done("ctx1")).then_inc(out_a, 1)
            for n in range(L // 4):
                if not by_vector(f"bias{n}"):
                    nc.scalar.copy(pos[:, :, 4 * n:4 * n + 4],
                                   done(f"bias{n}").rearrange("p (i r) -> p r i", i=4)).then_inc(out_a, 1)
            nc.scalar.mul(kc_t[:, 0:HT], done("kc0"), SCALE).then_inc(out_a, 1)
            nc.scalar.mul(kc_t[:, HT:], done("kc1"), SCALE).then_inc(out_a, 1)
            for f in range(2):
                nc.scalar.copy(v_aug[:, 1, f * HB:(f + 1) * HB, :, 0:HD].rearrange("p b h d -> p (b h) d"),
                               done(f"vc{f}").rearrange("p (n d) -> p n d", d=HD)).then_inc(out_a, 1)
            nc.scalar.copy(rw_t[:, :], done("w_router")[:, 0:E]).then_inc(out_a, 1)
            act.wait_ge(consts_made, 4)

            def exps(U):
                act.wait_ge(max_ready, U + 1)
                if U >= 3:
                    act.wait_ge(probst_ready, U - 2)
                for h4 in range(GH):
                    last = nc.scalar.activation(probs[:, U % 3, h4 * L:(h4 + 1) * L],
                                                ps[BS[U % 2]][:, h4 * L:(h4 + 1) * L], ACT.Exp,
                                                bias=neg_max[:, U % 4, h4:h4 + 1])
                last.then_inc(exp_done, 1)

            def probs_out(U):
                act.wait_ge(probst_ready, U + 1)
                if U >= 3:
                    act.wait_ge(pv_done, U - 2)
                nc.scalar.copy(probs_t[:, U % 3, :], ps[BP[U % 2]][:, :]).then_inc(pt_out_a, 1)

            def outputs_out(B):
                act.wait_ge(pv_done, NG * (B + 1))
                if B >= 2:
                    act.wait_ge(back_ready, B - 1)
                nc.scalar.copy(o_t[:, B % 2, :], ps[BO][:, :]).then_inc(ot_out, 1)

            def turned_out(B):
                act.wait_ge(ont_ready, B + 1)
                if B >= 2:
                    act.wait_ge(proj_ready, B - 1)
                nc.scalar.copy(on_t[:, B % 2, :], ps[BN][:, 0:128]).then_inc(ont_out, 1)

            def deviation(B):
                act.wait_ge(mom_ready, B + 1)
                link(nc.scalar.activation(ln_var[:, B % 2], moments[:, B % 2, 1:2], ACT.Ln, bias=eps_col[:, :]))
                nc.scalar.activation(rstd[:, B % 2], ln_var[:, B % 2], ACT.Exp, scale=-0.5).then_inc(rstd_ready, 1)

            def tokens_out(B):
                act.wait_ge(xt_ready, B + 1)
                b = B % NB
                if 2 <= B < NB:
                    act.wait_ge(q_ready, B - 1)
                if B == NB:
                    act.wait_ge(task_done, len(TASKS))
                dst = x1_t[:, b % 2, :] if B < NB else x2_t[:, b * L:(b + 1) * L]
                if B >= NB:
                    nc.scalar.copy(x2_hi[:, b * L:(b + 1) * L], ps[BN][:, 0:D])
                nc.scalar.copy(dst, ps[BN][:, 0:D]).then_inc(xt_out, 1)

            def queries_out(B):
                b = B % NB
                if B < NB:
                    act.wait_ge(q_ready, b + 1)
                    act.wait_ge(qk_ready, 2 * (b + 1))
                    nc.scalar.copy(qc_t[:, b * L:(b + 1) * L], ps[BX][:, 0:L]).then_inc(qc_out, 1)
                else:
                    act.wait_ge(logit_ready, b + 1)
                    if b in (HB, HB + 2):
                        act.wait_ge(exp_read, (b - HB) // 2 + 1)
                    nc.scalar.activation(r_exp[:, b % HB, :], ps[BX][:, 0:E], ACT.Exp, scale=-1.0)\
                        .then_inc(logit_exp, 1)

            def weights_out(f):
                act.wait_ge(ct_ready, f + 1)
                nc.scalar.copy(comb_t[:, f * HT:(f + 1) * HT], ps[BN][:, 0:HT // 2].bitcast(F16)).then_inc(ct_out, 1)

            def squares(k):
                act.wait_ge(h_ready, k + 1)
                if k == 0:
                    act.wait_ge(w_split, NB)
                else:
                    act.wait_ge(sq_ready, k)
                nc.scalar.activation(relu_sb[:, :], ps[BS[k % 2]][:, :], ACT.Relu).then_inc(relu_ready, 1)
                if k >= 2:
                    act.wait_ge(unit_ready, k - 1)
                act.wait_ge(relu_ready, k + 1)
                nc.scalar.activation(sq[:, k % 2], relu_sb[:, :], ACT.Square).then_inc(sq_ready, 1)

            def unit_high(k):
                act.wait_ge(unit_ready, k + 1)
                if k >= R:
                    act.wait_ge(down_done, k - R + 1)
                nc.scalar.copy(unit_hi[:, k % R], unit[:, k % 3]).then_inc(hi_ready_a, 1)

            def y_copy(f):
                act.wait_ge(down_done, (f + 1) * CH)
                if f == 1:
                    act.wait_ge(yback_ready, 1)
                nc.scalar.copy(y_t[:, :], ps[(BO, BN)[f]][:, :]).then_inc(y_out_t, 1)

            def y_deviation(f):
                act.wait_ge(ymom_ready, f + 1)
                link(nc.scalar.activation(y_ln[:, :], y_mom[:, :, 1], ACT.Ln, bias=eps_col[:, :]))
                nc.scalar.activation(y_rstd[:, :], y_ln[:, :], ACT.Exp, scale=-0.5).then_inc(yrstd_ready, 1)

            for s in range(STEPS):
                k = s - MOE0
                for m, part in ((M - 1, outputs_out), (M + TURN + 1, turned_out), (M + TOKENS + 1, tokens_out),
                                (M + USE + 1, queries_out)):
                    if (s - m) % NG == 0 and 0 <= (s - m) // NG < 2 * NB:
                        part((s - m) // NG)
                if s in CT:
                    weights_out(CT.index(s))
                if s < STAGES:
                    exps(s)
                if 0 <= s - LT < STAGES and not probs_by_vector(s - LT):
                    probs_out(s - LT)
                if 0 <= k < 2 * CH:
                    squares(k)
                if 1 <= k <= 2 * CH and not high_by_vector(k - 1):
                    unit_high(k - 1)
                if (s - M - PROJ - 1) % NG == 0 and 0 <= (s - M - PROJ - 1) // NG < 2 * NB:
                    deviation((s - M - PROJ - 1) // NG)
                if k == CH + LD:
                    y_copy(0)
                if k == CH + LD + 4:
                    y_deviation(0)
            y_copy(1)
            y_deviation(1)

        @block.vector
        def _(dve):
            chain = [0]

            def link(ins):
                chain[0] += 1
                ins.then_inc(v_chain, 1)
                dve.wait_ge(v_chain, chain[0])

            def done(task):
                dve.wait_ge(task_done, TASKS.index(task) + 1)
                return bank_of(task)[:, :]

            nc.vector.memset(ps[BO][:, :], 0.0).then_inc(bank_zero, 1)
            dve.wait_ge(masks_made, 1)
            nc.vector.tensor_reduce(slot_mask[:, :], head_mask[:, :].rearrange("p (g h) -> p h g", g=NG),
                                    AX.X, ALU.add).then_inc(groups_made, 1)
            nc.vector.tensor_reduce(group_mask[:, :], head_mask[:, :].rearrange("p (g h) -> p g h", g=NG),
                                    AX.X, ALU.add).then_inc(groups_made, 1)
            nc.vector.tensor_copy(w_t[:, :, :].rearrange("p c d -> p (c d)"), done("w_self")).then_inc(out_v, 1)
            dve.wait_ge(pads_made, 2)
            nc.vector.tensor_copy(rel_t[:, REL0:REL0 + NREL], done("rel")[:, 0:NREL]).then_inc(out_v, 1)

            def spread_queries(c):
                if c >= 2:
                    dve.wait_ge(task_done, TASKS.index(f"bias{8 * (c - 1) - 1}") + 1)
                src = q_t[:, 32 * NB * c:32 * NB * (c + 1)].rearrange("p (i b) -> p i b", b=NB)
                for h in range(H):
                    last = nc.vector.tensor_scalar(q_spread[:, c % 2, :, h * NB:(h + 1) * NB], src,
                                                   head_mask[:, h:h + 1], None, ALU.mult)
                last.then_inc(spread_ready, 1)

            def keys_out(half):
                nc.vector.tensor_scalar(k_t[:, half * HT:(half + 1) * HT], done(f"k{half}"), qkvb_col[:, 1:2], SCALE,
                                        ALU.add, ALU.mult).then_inc(out_v, 1)

            def values_out(half):
                nc.vector.tensor_tensor(v_aug[:, 0, half * HB:(half + 1) * HB, :, 0:HD],
                                        done(f"v{half}").rearrange("p (b h d) -> p b h d", b=HB, h=H),
                                        vb_row[:, :].rearrange("p (h d) -> p h d", h=H).unsqueeze(1)
                                        .broadcast_to([128, HB, H, HD]), ALU.add).then_inc(out_v, 1)

            def bias_out(n):
                nc.vector.tensor_tensor(pos[:, :, 4 * n:4 * n + 4], done(f"bias{n}").rearrange("p (i r) -> p r i", i=4),
                                        rel_mask[:, 4 * n:4 * n + 4].unsqueeze(1).broadcast_to([128, H * NB, 4]),
                                        ALU.add).then_inc(out_v, 1)

            dve.wait_ge(out_a, out_count("q0", False))
            spread_queries(0)
            dve.wait_ge(ld["qkvb"], 16)
            keys_out(0)
            keys_out(1)
            dve.wait_ge(ld["vb"], 16)
            values_out(0)
            values_out(1)
            spread_queries(1)
            dve.wait_ge(masks_made, 2)
            for n in range(L // 4):
                if n == 7:
                    dve.wait_ge(out_a, out_count("q1", False))
                if n in (7, 16):
                    spread_queries(2 + (n > 8))
                if by_vector(f"bias{n}"):
                    bias_out(n)

            def maxima(U):
                dve.wait_ge(scores_ready, U + 1)
                if U >= 4:
                    dve.wait_ge(exp_done, U - 3)
                nc.vector.tensor_reduce(neg_max[:, U % 4, :], ps[BS[U % 2]][:, :].rearrange("p (h j) -> p h j", h=GH),
                                        AX.X, ALU.max, negate=True).then_inc(max_ready, 1)

            def probs_out(U):
                dve.wait_ge(probst_ready, U + 1)
                if U >= 3:
                    dve.wait_ge(pv_done, U - 2)
                nc.vector.tensor_copy(probs_t[:, U % 3, :], ps[BP[U % 2]][:, :]).then_inc(pt_out_v, 1)

            def normalise(B):
                dve.wait_ge(back_ready, B + 1)
                if B >= 2:
                    dve.wait_ge(ont_ready, B - 1)
                o = ps[BM][:, :].rearrange("p (h c) -> p h c", h=H)
                link(nc.vector.reciprocal(rden[:, B % 2, :], o[:, :, HD]))
                nc.vector.tensor_tensor(o_norm[:, B % 2, :].rearrange("p (h d) -> p h d", h=H), o[:, :, 0:HD],
                                        rden[:, B % 2, :].unsqueeze(2).broadcast_to([128, H, HD]), ALU.mult)\
                    .then_inc(on_ready, 1)

            def residual(B):
                dve.wait_ge(proj_ready, B + 1)
                if B == 0:
                    dve.wait_ge(xb_made, 1)
                base = (x_tok if B < NB else x1_tok)[:, B % NB, :]
                link(nc.vector.tensor_tensor(res[:, B % 2, :], ps[BX][:, 0:D], base, ALU.add))
                link(nc.vector.bn_stats(stats[:, B % 2, :], res[:, B % 2, :]))
                nc.vector.bn_aggr(moments[:, B % 2, :], stats[:, B % 2, :]).then_inc(mom_ready, 1)

            def layer_norm(B):
                dve.wait_ge(rstd_ready, B + 1)
                dst = (x1_tok if B < NB else x2_tok)[:, B % NB, :]
                nc.vector.tensor_scalar(dst, res[:, B % 2, :], moments[:, B % 2, 0:1], rstd[:, B % 2, :],
                                        ALU.subtract, ALU.mult).then_inc(x_norm, 1)

            def route(q, part):
                seqs = BATCHES[q][0]
                size, first = len(seqs), seqs[0] % HB
                all_n = slice(first, first + size)
                if part == 0:
                    dve.wait_ge(logit_exp, seqs[-1] + 1)
                    dve.wait_ge(ld["corr"], 16)
                    nc.vector.tensor_scalar(r_one[:, all_n, :], r_exp[:, all_n, :], 1.0, None, ALU.add)\
                        .then_inc(exp_read, 1)
                    dve.wait_ge(exp_read, q + 1)
                    link(nc.vector.reciprocal(score[:, all_n, :], r_one[:, all_n, :]))
                    link(nc.vector.tensor_tensor(biased[:, all_n, :], score[:, all_n, :],
                                                 corr_row[:, :].unsqueeze(1).broadcast_to([128, size, E]), ALU.add))
                if part in (1, 2):
                    for n in range(first + (part - 1) * size // 2, first + part * size // 2):
                        for g in range(EG):
                            last = nc.vector.max(top_in[:, n, g, :], biased[:, n, g * ES:(g + 1) * ES])
                    link(last)
                if part == 3:
                    link(nc.vector.tensor_tensor(gscore[:, all_n, 0:EG],
                                                 top_in[:, all_n, :, 0], top_in[:, all_n, :, 1], ALU.add))
                    for n in range(first, first + size):
                        last = nc.vector.max(gtop[:, n, :], gscore[:, n, 0:EG])
                    link(last)
                    link(nc.vector.tensor_copy(glist[:, all_n, 0:TOPG], gtop[:, all_n, 0:TOPG]))
                if part == 4:
                    for n in range(first, first + size):
                        last = nc.vector.match_replace(grep[:, n, :], glist[:, n, :], gscore[:, n, :], 3.0e38)
                    link(last)
                    link(nc.vector.tensor_tensor(gkeep[:, all_n, :], grep[:, all_n, 0:EG],
                                                 gscore[:, all_n, 0:EG], ALU.not_equal))
                    link(nc.vector.tensor_tensor(
                        masked[:, all_n, :].rearrange("p n (g e) -> p (n g) e", g=EG),
                        biased[:, all_n, :].rearrange("p n (g e) -> p (n g) e", g=EG),
                        gkeep[:, all_n, :].rearrange("p n g -> p (n g)").unsqueeze(2).broadcast_to([128, size * EG, ES]),
                        ALU.mult))
                if part == 5:
                    for n in range(first, first + size):
                        last = nc.vector.max(etop[:, n, :], masked[:, n, :])
                    link(last)
                    for n in range(first, first + size):
                        last = nc.vector.match_replace(erep[:, n, :], etop[:, n, :], masked[:, n, :], 3.0e38)
                    link(last)
                    link(nc.vector.tensor_tensor(chosen[:, all_n, :], erep[:, all_n, :], masked[:, all_n, :], ALU.not_equal))
                if part == 6:
                    link(nc.vector.tensor_tensor(weight[:, all_n, :], score[:, all_n, :], chosen[:, all_n, :], ALU.mult))
                    link(nc.vector.tensor_reduce(wsum[:, all_n], weight[:, all_n, :], AX.X, ALU.add))
                    link(nc.vector.tensor_scalar(wsum1[:, all_n], wsum[:, all_n], 1e-20, None, ALU.add))
                    link(nc.vector.reciprocal(wrec[:, all_n], wsum1[:, all_n]))
                if part == 7:
                    if q >= 2:
                        dve.wait_ge(ct_ready, 1)
                    for n in range(first, first + size):
                        last = nc.vector.tensor_scalar(comb[:, n, :], weight[:, n, :], wrec[:, n:n + 1], ROUTE_SCALE,
                                                       ALU.mult, ALU.mult)
                    link(last)
                    link(nc.vector.tensor_copy(comb_split[:, all_n, 0, :], comb[:, all_n, :]))
                    link(nc.vector.tensor_tensor(comb_rest[:, all_n, :], comb[:, all_n, :], comb_split[:, all_n, 0, :],
                                                 ALU.subtract))
                    nc.vector.tensor_scalar(comb_split[:, all_n, 1, :], comb_rest[:, all_n, :], LO, None, ALU.mult)\
                        .then_inc(comb_ready, 1)

            def split_weights(n):
                dve.wait_ge(w_high, n + 1)
                if n == 0:
                    nc.vector.tensor_tensor(sh_lo[:, :, :], shared[:, :, :], sh_hi[:, :, :], ALU.subtract)
                way, cols = piece(n)
                nc.vector.tensor_tensor(w_lo[:, way, cols], experts[:, way, cols], w_hi[:, way, cols],
                                        ALU.subtract).then_inc(w_split, 1)

            def split_tokens(b):
                cols = slice(b * L, (b + 1) * L)
                dve.wait_ge(xt_out, NB + b + 1)
                nc.vector.tensor_tensor(x2_lo[:, cols], x2_t[:, cols], x2_hi[:, cols], ALU.subtract)\
                    .then_inc(x2_split, 1)

            def units(k):
                f, c = k // CH, k % CH - NSH
                dve.wait_ge(sq_ready, k + 1)
                if k >= 3:
                    wait_rest(dve, k - 3)
                if c >= 0:
                    n = f * NPAIR + c
                    dve.wait_ge(c_ready, n + 1)
                    ins = nc.vector.tensor_tensor(unit[:, k % 3], ps[BP[n % 2]][:, :], sq[:, k % 2], ALU.mult)
                else:
                    ins = nc.vector.tensor_copy(unit[:, k % 3], sq[:, k % 2])
                ins.then_inc(unit_ready, 1)

            def units_high(k):
                dve.wait_ge(unit_ready, k + 1)
                if k >= R:
                    dve.wait_ge(down_done, k - R + 1)
                nc.vector.tensor_copy(unit_hi[:, k % R], unit[:, k % 3]).then_inc(hi_ready_v, 1)

            def units_rest(k):
                wait_high(dve, k)
                if k >= R:
                    dve.wait_ge(down_done, k - R + 1)
                nc.vector.tensor_tensor(unit_lo[:, k % R], unit[:, k % 3], unit_hi[:, k % R],
                                        ALU.subtract).then_inc(lo_ready_v, 1)

            def y_residual(f):
                dve.wait_ge(yback_ready, f + 1)
                if f:
                    dve.wait_ge(yrstd_ready, 1)
                link(nc.vector.tensor_tensor(y_res[:, :, :].rearrange("p n d -> p (n d)"), ps[BM][:, :],
                                             x2_tok[:, f * HB:(f + 1) * HB, :].rearrange("p n d -> p (n d)"), ALU.add))
                for n in range(HB):
                    last = nc.vector.bn_stats(y_stats[:, n, :], y_res[:, n, :])
                link(last)
                for n in range(HB):
                    last = nc.vector.bn_aggr(y_mom[:, n, :], y_stats[:, n, :])
                last.then_inc(ymom_ready, 1)

            def y_norm(f):
                dve.wait_ge(yrstd_ready, f + 1)
                for n in range(HB):
                    last = nc.vector.tensor_scalar(y_out[:, f * HB + n, :], y_res[:, n, :], y_mom[:, n, 0:1],
                                                   y_rstd[:, n:n + 1], ALU.subtract, ALU.mult)
                last.then_inc(y_done, 1)

            for s in range(STEPS):
                k = s - MOE0
                for m, part in ((M + BACK + 1, normalise), (M + PROJ + 1, residual), (M + NORM, layer_norm)):
                    if (s - m) % NG == 0 and 0 <= (s - m) // NG < 2 * NB:
                        part((s - m) // NG)
                if s < STAGES:
                    maxima(s)
                if 0 <= s - LT < STAGES and probs_by_vector(s - LT):
                    probs_out(s - LT)
                if 0 <= k < 2 * CH:
                    units(k)
                for q, (_, rate) in enumerate(BATCHES):
                    for part in range(PARTS):
                        if s - ROUTE0[q] == int(part / rate):
                            route(q, part)
                if (s - NG * NB - 2) % NG == 0 and 0 <= (s - NG * NB - 2) // NG < NB:
                    split_weights((s - NG * NB - 2) // NG)
                if (s - M - TOKENS - 2) % NG == 0 and NB <= (s - M - TOKENS - 2) // NG < 2 * NB:
                    split_tokens((s - M - TOKENS - 2) // NG - NB)
                if k == CH + LD + 3:
                    y_residual(0)
                if k == CH + LD + 5:
                    y_norm(0)
                if 1 <= k <= 2 * CH and not rest_by_pool(k - 1):
                    units_rest(k - 1)
                if 0 <= k < 2 * CH and high_by_vector(k):
                    units_high(k)
            y_residual(1)
            y_norm(1)


_INS = ["x", "ctx_1024", "L0_attn_qkv_w", "L0_attn_qkv_b", "L0_attn_proj_w", "L0_attn_proj_b", "L0_attn_rel_emb",
        "L0_xattn_wq", "L0_xattn_wk", "L0_xattn_wv", "L0_xattn_wo", "L0_ffn_router_w", "L0_ffn_correction_bias",
        "L0_ffn_up_w", "L0_ffn_down_w", "L0_ffn_shared_up_w", "L0_ffn_shared_down_w"]


def kernel(**inputs):
    import numpy as _np
    import concourse.bacc as _bacc
    from concourse import mybir as _mybir
    from concourse.bass_utils import run_bass_kernel_spmd as _run

    nc = _bacc.Bacc("TRN2", target_bir_lowering=False, num_devices=1)
    arrays, args = {}, []
    for name in _INS:
        a = _np.ascontiguousarray(inputs[name])
        arrays[f"in_{name}"] = a
        args.append(nc.dram_tensor(f"in_{name}", a.shape, _mybir.dt.from_np(a.dtype), kind="ExternalInput").ap())
    args.append(nc.dram_tensor("out_0", (NB, L, D), F32, kind="ExternalOutput").ap())
    decoder_layer(nc, *args)
    r = _run(nc, [arrays], core_ids=[0])
    return r.results[0]["out_0"]
```

```python
from contextlib import ExitStack

import concourse.bass as bass
from concourse import mybir

F32 = mybir.dt.float32
BF16 = mybir.dt.bfloat16
F16 = mybir.dt.float16
F32R = mybir.dt.float32r
ALU = mybir.AluOpType
ACT = mybir.ActivationFunctionType
AX = mybir.AxisListType

NB, L, D = 8, 128, 128
H, HD = 16, 8
NG, GH = 4, 4
MAX_REL = 100
NREL = 2 * MAX_REL - 1
REL0 = L - MAX_REL
NEG = 1.0e8
CAUSAL = -1.0e30
SCALE = float(HD) ** -0.5
EPS = 1e-5
E, TOPK, EG, TOPG = 64, 8, 8, 4
ES = E // EG
IM = 64
NPAIR = E // 2
NSH = 2
ROUTE_SCALE = 2.5
LO = 4096.0
HB = 4
HT = HB * L
NV = HD + 1

NU = NB * NG
STAGES = 2 * NU
LT = 2
LV = LT + 1
M = LV + NG + 1
MOE0 = STAGES + LV
CH = NPAIR + NSH
LD = 4
STEPS = MOE0 + 2 * CH + LD
R = LD + 1
PARTS = 14
BACK, TURN, PROJ, TOKENS, USE = 0, 2, 4, 8, 10
NORM = 7
BATCHES = [(range(0, 2), 2), (range(2, 4), 3.5), (range(4, 8), 0.875)]
ROUTE0 = [NG * (NB + seqs[-1]) + M + USE + 2 for seqs, _ in BATCHES]
CT = [ROUTE0[1] + 5, ROUTE0[2] + 17]

BY_POOL = 6
REST2 = 2 * NB

BS, BX, BP, BO, BM, BN = (1, 4, 0), 2, 3, 5, 6, 7
BH, BC = (0, 1), (3, 4)
PREP_BANKS = [0, 1, 2, 3, 4, 6, 7]
TASKS = (["w_self", "x0", "x1", "q0", "q1", "rel", "k0", "k1", "v0", "v1", "w_cross", "ctx0", "ctx1",
          "vc0", "vc1", "w_router"]
         + [f"bias{n}" for n in range(L // 4)]
         + ["kc0", "kc1"])


def by_vector(task):
    if task.startswith("bias"):
        i = 4 * int(task[4:])
        return i < REL0 or i >= MAX_REL
    return task in ("w_self", "rel", "v0", "v1")


def out_count(task, vector):
    return sum(by_vector(t) == vector for t in TASKS[:TASKS.index(task) + 1])


def piece(n):
    size = 2 * E * IM // NB
    return n // (NB // 2), slice(n % (NB // 2) * size, (n % (NB // 2) + 1) * size)


def probs_by_vector(U):
    return U % (2 if U < NU else 4) == 0


def probs_copied(U):
    v = probs_by_vector(U)
    return v, sum(probs_by_vector(n) == v for n in range(U + 1))


def decoder_layer(nc, x, ctx_in, qkv_w, qkv_b, proj_w, proj_b, rel_emb, wq, wk, wv, wo,
                  router_w, corr, up_w, down_w, sh_up, sh_down, out):
    with ExitStack() as ctx:
        def sb(name, shape, dt=F32):
            return ctx.enter_context(nc.sbuf_tensor(name, shape, dt))

        def sem(name):
            return ctx.enter_context(nc.semaphore(name))

        ps = [ctx.enter_context(nc.psum_tensor(f"bank{n}", [128, 512], F32)) for n in range(8)]

        with ExitStack() as first:
            def sb1(name, shape, dt=F32):
                return first.enter_context(nc.sbuf_tensor(name, shape, dt))

            pos = sb1("pos", [128, H * NB, L])
            k_t = sb1("k_t", [128, NB * L])
            ctx_t = sb1("ctx_t", [128, NB * L])
            w_raw = sb1("w_raw", [128, 4, D])
            wc_raw = sb1("wc_raw", [128, 4, D])
            spread = sb1("spread", [128, 2 * 32 * 128])
        q_spread = spread[:, :].rearrange("p (r i n) -> p r i n", r=2, i=32)
        w_hi = sb("w_hi", [128, 2, E * IM], F32R)
        w_lo = sb("w_lo", [128, 2, E * IM], F32R)
        x2_hi = sb("x2_hi", [128, NB * L], F32R)
        x2_lo = sb("x2_lo", [128, NB * L], F32R)
        sh_hi = sb("sh_hi", [128, 2, NSH * 128], F32R)
        sh_lo = sb("sh_lo", [128, 2, NSH * 128], F32R)
        with ExitStack() as second:
            def sb2(name, shape, dt=F32):
                return second.enter_context(nc.sbuf_tensor(name, shape, dt))

            k_bd = sb2("k_bd", [128, 2, 2, GH, L], F32R)
            q_bd = sb2("q_bd", [128, 2, 2, NG, L], F32R)
            kc_hi = sb2("kc_hi", [128, NB * L])
            incoming = sb2("incoming", [128, 2, 2 * E * IM // NB])
        relu_sb = sb("relu_sb", [128, HT])
        sq = sb("sq", [128, 2, HT])
        unit = sb("unit", [128, 3, HT])
        unit_hi = sb("unit_hi", [128, R, HT], F32R)
        unit_lo = sb("unit_lo", [128, R, HT], F32R)

        ident = sb("ident", [128, 128])
        identb = sb("identb", [128, 128], BF16)
        ident_h = sb("ident_h", [128, 128], F16)
        head_mask = sb("head_mask", [128, H])
        slot_mask = sb("slot_mask", [128, GH])
        group_mask = sb("group_mask", [128, NG])
        rel_mask = sb("rel_mask", [128, L])
        causal = sb("causal", [128, L], BF16)
        select = sb("select", [128, NPAIR, 2, IM], F16)
        x_tok = sb("x_tok", [128, NB, D])
        ctx_tok = sb("ctx_tok", [128, NB, D])
        rw_raw = sb("rw_raw", [E, D])
        rel_raw = sb("rel_raw", [128, 2, D])
        qkvb_col = sb("qkvb_col", [128, 3])
        kb_col = sb("kb_col", [128, 1])
        vb_row = sb("vb_row", [128, D])
        pb_row = sb("pb_row", [128, D])
        corr_row = sb("corr_row", [128, E])
        shared = sb("shared", [128, 2, NSH * 128])
        w_t = sb("w_t", [128, 4, D])
        wc_t = sb("wc_t", [128, 4, D])
        rw_t = sb("rw_t", [128, E])
        rel_t = sb("rel_t", [128, 2 * L])
        x_t = sb("x_t", [128, NB * L])
        q_t = sb("q_t", [128, NB * L])
        kc_t = sb("kc_t", [128, NB * L])
        v_aug = sb("v_aug", [128, 2, NB, H, NV])
        k_hi = sb("k_hi", [128, NB * L])
        q_hi = sb("q_hi", [128, NB * L])
        qc_t = q_t
        probs = sb("probs", [128, 3, 512])
        probs_t = sb("probs_t", [128, 3, 512])
        neg_max = sb("neg_max", [128, 4, GH])
        o_t = sb("o_t", [128, 2, 512])
        rden = sb("rden", [128, 2, H])
        o_norm = sb("o_norm", [128, 2, D])
        on_t = sb("on_t", [128, 2, D])
        res = sb("res", [128, 2, D])
        stats = sb("stats", [128, 2, 6])
        moments = sb("moments", [128, 2, 2])
        ln_var = sb("ln_var", [128, 2, 1])
        rstd = sb("rstd", [128, 2, 1])
        eps_col = sb("eps_col", [128, 1])
        x1_tok = x2_tok = x_tok
        x1_t = sb("x1_t", [128, 2, L])
        x2_t = x_t
        r_exp = sb("r_exp", [128, HB, E])
        r_one = sb("r_one", [128, HB, E])
        score = sb("score", [128, HB, E])
        biased = sb("biased", [128, HB, E])
        top_in = sb("top_in", [128, HB, EG, 8])
        gscore = sb("gscore", [128, HB, 16])
        gtop = sb("gtop", [128, HB, 8])
        glist = sb("glist", [128, HB, 8])
        grep = sb("grep", [128, HB, 16])
        gkeep = sb("gkeep", [128, HB, EG])
        masked = sb("masked", [128, HB, E])
        etop = sb("etop", [128, HB, 8])
        erep = sb("erep", [128, HB, E])
        chosen = sb("chosen", [128, HB, E])
        weight = sb("weight", [128, HB, E])
        wsum = sb("wsum", [128, HB])
        wsum1 = sb("wsum1", [128, HB])
        wrec = sb("wrec", [128, HB])
        comb = sb("comb", [128, HB, E])
        comb_rest = sb("comb_rest", [128, HB, E])
        comb_split = sb("comb_split", [128, HB, 2, E], F16)
        comb_t = sb("comb_t", [128, NB * L], F16)
        y_t = sb("y_t", [128, HT])
        y_res = sb("y_res", [128, HB, D])
        y_stats = sb("y_stats", [128, HB, 6])
        y_mom = sb("y_mom", [128, HB, 2])
        y_ln = sb("y_ln", [128, HB])
        y_rstd = sb("y_rstd", [128, HB])
        y_out = ctx_tok

        loads = ["x0", "x1", "w", "w2", "rel", "rel2", "qkvb", "vb", "pb", "ctx", "c0", "c1", "c2", "c3", "rw", "corr",
                 "sup", "sdn", "piece0", "piece1"]
        ld = {n: sem(f"ld_{n}") for n in loads}
        ident_made = sem("ident_made")
        masks_made = sem("masks_made")
        consts_made = sem("consts_made")
        pads_made = sem("pads_made")
        xb_made = sem("xb_made")
        pool_chain = sem("pool_chain")
        shared_high = sem("shared_high")
        w_high = sem("w_high")
        w_split_p = sem("w_split_p")
        lo_ready = sem("lo_ready")
        qk_ready = sem("qk_ready")
        task_done = sem("task_done")
        scores_ready = sem("scores_ready")
        probst_ready = sem("probst_ready")
        pv_done = sem("pv_done")
        back_ready = sem("back_ready")
        ont_ready = sem("ont_ready")
        proj_ready = sem("proj_ready")
        xt_ready = sem("xt_ready")
        q_ready = sem("q_ready")
        logit_ready = sem("logit_ready")
        ct_ready = sem("ct_ready")
        h_ready = sem("h_ready")
        c_ready = sem("c_ready")
        down_done = sem("down_done")
        y_ready = sem("y_ready")
        yback_ready = sem("yback_ready")
        heads_split = sem("heads_split")
        qc_split = sem("qc_split")
        bank_zero = sem("bank_zero")
        out_v = sem("out_v")
        groups_made = sem("groups_made")
        spread_ready = sem("spread_ready")
        v_chain = sem("v_chain")
        max_ready = sem("max_ready")
        pt_out_v = sem("pt_out_v")
        on_ready = sem("on_ready")
        mom_ready = sem("mom_ready")
        x_norm = sem("x_norm")
        exp_read = sem("exp_read")
        comb_ready = sem("comb_ready")
        unit_ready = sem("unit_ready")
        hi_ready = sem("hi_ready")
        w_split_v = sem("w_split_v")
        x2_split = sem("x2_split")
        ymom_ready = sem("ymom_ready")
        y_done = sem("y_done")
        out_a = sem("out_a")
        a_chain = sem("a_chain")
        exp_done = sem("exp_done")
        pt_out_a = sem("pt_out_a")
        ot_out = sem("ot_out")
        ont_out = sem("ont_out")
        rstd_ready = sem("rstd_ready")
        xt_out = sem("xt_out")
        qc_out = sem("qc_out")
        logit_exp = sem("logit_exp")
        ct_out = sem("ct_out")
        relu_ready = sem("relu_ready")
        sq_ready = sem("sq_ready")
        y_out_t = sem("y_out_t")
        yrstd_ready = sem("yrstd_ready")
        stored = sem("stored")

        block = ctx.enter_context(nc.Block())

        def bank_of(task):
            return ps[PREP_BANKS[TASKS.index(task) % len(PREP_BANKS)]]

        def wait_split(eng, n):
            eng.wait_ge(w_split_v, min(n + 1, BY_POOL))
            if n >= BY_POOL:
                eng.wait_ge(w_split_p, n + 1 - BY_POOL)

        @block.sync
        def _(sp):
            sp.dma_start(w_raw[:, 0:3, :], qkv_w.rearrange("(c r) d -> r c d", r=128)).then_inc(ld["w"], 16)
            sp.dma_start(w_raw[:, 3, :], proj_w).then_inc(ld["w2"], 16)
            for f in range(2):
                sp.dma_start(x_tok[:, f * HB:(f + 1) * HB, :],
                             x[f * HB:(f + 1) * HB].rearrange("b i d -> i b d")).then_inc(ld[f"x{f}"], 16)
            sp.dma_start(qkvb_col[:, :], qkv_b.rearrange("(c r) -> r c", r=128),
                         allow_slow_non_contiguous=True).then_inc(ld["qkvb"], 16)
            rel_v = rel_emb.rearrange("h m d -> m h d")
            sp.dma_start(rel_raw[:, 0, :].rearrange("m (h d) -> m h d", h=H), rel_v[0:128]).then_inc(ld["rel"], 16)
            sp.dma_start(rel_raw[0:NREL - 128, 1, :].rearrange("m (h d) -> m h d", h=H),
                         rel_v[128:NREL]).then_inc(ld["rel2"], 16)
            sp.dma_start(ctx_tok[:, :, :], ctx_in.rearrange("b i d -> i b d")).then_inc(ld["ctx"], 16)
            sp.dma_start(vb_row[:, :], qkv_b[2 * D:3 * D].partition_broadcast(128)).then_inc(ld["vb"], 16)
            for n, w in enumerate((wq, wk, wv, wo)):
                sp.dma_start(wc_raw[:, n, :], w).then_inc(ld[f"c{n}"], 16)
            sp.dma_start(pb_row[:, :], proj_b.partition_broadcast(128)).then_inc(ld["pb"], 16)
            sp.dma_start(rw_raw[:, :], router_w).then_inc(ld["rw"], 16)
            sp.dma_start(corr_row[:, :], corr.partition_broadcast(128)).then_inc(ld["corr"], 16)
            sp.dma_start(shared[:, 0, :], sh_up).then_inc(ld["sup"], 16)
            sp.dma_start(shared[:, 1, :].rearrange("p (c d) -> p c d", c=NSH),
                         sh_down.rearrange("(c i) d -> i c d", c=NSH)).then_inc(ld["sdn"], 16)
            for n in range(NB):
                if n == 0:
                    sp.wait_ge(task_done, TASKS.index(f"bias{L // 4 - 1}") + 1)
                if n >= 2:
                    wait_split(sp, n - 2)
                way, cols = piece(n)
                if way == 0:
                    sp.dma_start(incoming[:, n % 2, :].rearrange("p (e i) -> p e i", i=IM),
                                 up_w[cols.start // IM:cols.stop // IM].rearrange("e d i -> d e i"))\
                        .then_inc(ld[f"piece{n % 2}"], 16)
                else:
                    sp.dma_start(incoming[:, n % 2, :].rearrange("p (c d) -> p c d", d=D),
                                 down_w.rearrange("(c e) i d -> (e i) c d", e=2)[:, cols.start // D:cols.stop // D])\
                        .then_inc(ld[f"piece{n % 2}"], 16)
            for f in range(2):
                sp.wait_ge(y_done, f + 1)
                sp.dma_start(out[f * HB:(f + 1) * HB].rearrange("b i d -> i b d"),
                             y_out[:, f * HB:(f + 1) * HB, :]).then_inc(stored, 16)
            sp.wait_ge(stored, 32)

        @block.gpsimd
        def _(pool):
            chain = [0]

            def link(ins):
                chain[0] += 1
                ins.then_inc(pool_chain, 1)
                pool.wait_ge(pool_chain, chain[0])

            link(nc.gpsimd.memset(ident[:, :], 0.0))
            nc.gpsimd.affine_select(out=ident[:, :], in_=ident[:, :], compare_op=ALU.not_equal, fill=1.0,
                                    base=0, pattern=[[-1, 128]], channel_multiplier=1).then_inc(ident_made, 1)
            pool.wait_ge(ident_made, 1)
            nc.gpsimd.tensor_copy(identb[:, :], ident[:, :]).then_inc(pads_made, 1)
            nc.gpsimd.tensor_copy(ident_h[:, :], ident[:, :]).then_inc(pads_made, 1)
            link(nc.gpsimd.memset(head_mask[:, :], 1.0))
            link(nc.gpsimd.affine_select(out=head_mask[:, :], in_=head_mask[:, :], compare_op=ALU.is_ge, fill=0.0,
                                         base=0, pattern=[[-HD, H]], channel_multiplier=1))
            nc.gpsimd.affine_select(out=head_mask[:, :], in_=head_mask[:, :], compare_op=ALU.is_ge, fill=0.0,
                                    base=HD - 1, pattern=[[HD, H]], channel_multiplier=-1).then_inc(masks_made, 1)
            nc.gpsimd.memset(rel_t[:, :], 0.0).then_inc(pads_made, 1)
            nc.gpsimd.memset(v_aug[:, :, :, :, HD:NV], 1.0).then_inc(pads_made, 1)
            link(nc.gpsimd.memset(rel_mask[:, :], 0.0))
            link(nc.gpsimd.affine_select(out=rel_mask[:, :], in_=rel_mask[:, :], compare_op=ALU.is_ge, fill=-NEG,
                                         base=MAX_REL - 1, pattern=[[1, L]], channel_multiplier=-1))
            nc.gpsimd.affine_select(out=rel_mask[:, :], in_=rel_mask[:, :], compare_op=ALU.is_ge, fill=-NEG,
                                    base=MAX_REL - 1, pattern=[[-1, L]], channel_multiplier=1).then_inc(masks_made, 1)
            link(nc.gpsimd.memset(causal[:, :], 0.0))
            nc.gpsimd.affine_select(out=causal[:, :], in_=causal[:, :], compare_op=ALU.is_ge, fill=CAUSAL,
                                    base=0, pattern=[[-1, L]], channel_multiplier=1).then_inc(consts_made, 1)
            nc.gpsimd.memset(eps_col[:, :], EPS).then_inc(consts_made, 1)
            nc.gpsimd.memset(gscore[:, :, 8:16], -3.0e38).then_inc(consts_made, 1)
            nc.gpsimd.memset(glist[:, :, TOPG:8], -3.0e38).then_inc(consts_made, 1)
            pool.wait_ge(ld["x0"], 16)
            pool.wait_ge(ld["x1"], 16)
            pool.wait_ge(ld["pb"], 16)
            pool.wait_ge(task_done, TASKS.index("x1") + 1)
            nc.gpsimd.tensor_tensor(x_tok[:, :, :], x_tok[:, :, :],
                                    pb_row[:, :].unsqueeze(1).broadcast_to([128, NB, D]), ALU.add).then_inc(xb_made, 1)

            for B in range(2 * NB):
                b, r = B % NB, B % 2
                cols = slice(b * L, (b + 1) * L)
                if B >= 2:
                    pool.wait_ge(scores_ready, 4 * (B - 1))
                if B == 0:
                    pool.wait_ge(groups_made, 2)
                    pool.wait_ge(task_done, TASKS.index(f"bias{L * 3 // 16 - 1}") + 1)
                if B in (0, NB):
                    pool.wait_ge(heads_split, 2 if B == 0 else 3)
                for part, keys in enumerate((k_hi if B < NB else kc_hi, k_t if B < NB else kc_t)):
                    nc.gpsimd.tensor_tensor(k_bd[:, part, r], keys[:, cols].unsqueeze(1).broadcast_to([128, GH, L]),
                                            slot_mask[:, :].unsqueeze(2).broadcast_to([128, GH, L]),
                                            ALU.mult).then_inc(qk_ready, 1)
                if B >= NB:
                    pool.wait_ge(qc_split, b + 1)
                for part, queries in enumerate((q_hi, q_t)):
                    nc.gpsimd.tensor_tensor(q_bd[:, part, r], queries[:, cols].unsqueeze(1).broadcast_to([128, NG, L]),
                                            group_mask[:, :].unsqueeze(2).broadcast_to([128, NG, L]),
                                            ALU.mult).then_inc(qk_ready, 1)
                if B >= NB:
                    if b == 0:
                        pool.wait_ge(ld["sup"], 16)
                        pool.wait_ge(ld["sdn"], 16)
                        pool.wait_ge(scores_ready, NU)
                        nc.gpsimd.tensor_copy(sh_hi[:, :, :], shared[:, :, :]).then_inc(shared_high, 1)
                    way, cols = piece(b)
                    pool.wait_ge(ld[f"piece{b % 2}"], 16 * (b // 2 + 1))
                    nc.gpsimd.tensor_copy(w_hi[:, way, cols], incoming[:, b % 2]).then_inc(w_high, 1)
                    if b >= BY_POOL:
                        pool.wait_ge(w_high, b + 1)
                        nc.gpsimd.tensor_tensor(w_lo[:, way, cols], incoming[:, b % 2], w_hi[:, way, cols],
                                                ALU.subtract).then_inc(w_split_p, 1)
                if B < NB:
                    n = NPAIR // NB
                    some, at = select[:, B * n:(B + 1) * n], -2 * B * n
                    link(nc.gpsimd.memset(some, 0.0))
                    link(nc.gpsimd.affine_select(out=some, in_=some, compare_op=ALU.not_equal, fill=1.0, base=at,
                                                 pattern=[[-2, n], [-1, 2], [0, IM]], channel_multiplier=1))
                    nc.gpsimd.affine_select(out=some, in_=some, compare_op=ALU.not_equal, fill=1.0 / LO,
                                            base=at - E, pattern=[[-2, n], [-1, 2], [0, IM]],
                                            channel_multiplier=1).then_inc(consts_made, 1)

            for k in range(-1, 2 * CH):
                if k in (-1, REST2):
                    for b in range(0 if k < 0 else HB, HB if k < 0 else NB):
                        cols = slice(b * L, (b + 1) * L)
                        pool.wait_ge(xt_out, NB + b + 1)
                        nc.gpsimd.tensor_tensor(x2_lo[:, cols], x2_t[:, cols], x2_hi[:, cols],
                                                ALU.subtract).then_inc(x2_split, 1)
                if k >= 0:
                    pool.wait_ge(hi_ready, k + 1)
                    if k >= R:
                        pool.wait_ge(down_done, k - R + 1)
                    nc.gpsimd.tensor_tensor(unit_lo[:, k % R], unit[:, k % 3], unit_hi[:, k % R],
                                            ALU.subtract).then_inc(lo_ready, 1)

        @block.tensor
        def _(pe):
            def start(task):
                n = TASKS.index(task)
                if n >= len(PREP_BANKS):
                    before = TASKS[n - len(PREP_BANKS)]
                    v = by_vector(before)
                    pe.wait_ge(out_v if v else out_a, out_count(before, v))

            def transposes(task, blocks, rows=128):
                start(task)
                for n, src in enumerate(blocks):
                    cols = src.shape[0]
                    last = nc.tensor.transpose(bank_of(task)[:, n * 128:n * 128 + cols], src, ident[0:cols, 0:cols])
                last.then_inc(task_done, 1)

            def project(task, w, src, half):
                start(task)
                nc.tensor.matmul(bank_of(task)[:, :], w, src[:, half * HT:(half + 1) * HT],
                                 start=True, stop=True).then_inc(task_done, 1)

            def values(task, w, src, half):
                start(task)
                for n in range(HB):
                    b = half * HB + n
                    last = nc.tensor.matmul(bank_of(task)[:, n * D:(n + 1) * D], src[:, b * L:(b + 1) * L], w,
                                            start=True, stop=True)
                last.then_inc(task_done, 1)

            pe.wait_ge(ident_made, 1)
            pe.wait_ge(ld["w"], 16)
            pe.wait_ge(ld["w2"], 16)
            transposes("w_self", [w_raw[:, n, :] for n in range(4)])
            pe.wait_ge(ld["x0"], 16)
            transposes("x0", [x_tok[:, b, :] for b in range(HB)])
            pe.wait_ge(ld["x1"], 16)
            transposes("x1", [x_tok[:, b, :] for b in range(HB, NB)])
            pe.wait_ge(out_v, out_count("w_self", True))
            pe.wait_ge(out_a, out_count("x0", False))
            project("q0", w_t[:, 0, :], x_t, 0)
            pe.wait_ge(out_a, out_count("x1", False))
            project("q1", w_t[:, 0, :], x_t, 1)
            pe.wait_ge(ld["rel"], 16)
            pe.wait_ge(ld["rel2"], 16)
            transposes("rel", [rel_raw[:, 0, :], rel_raw[0:NREL - 128, 1, :]])
            project("k0", w_t[:, 1, :], x_t, 0)
            project("k1", w_t[:, 1, :], x_t, 1)
            values("v0", w_t[:, 2, :], x_t, 0)
            values("v1", w_t[:, 2, :], x_t, 1)
            for n in range(4):
                pe.wait_ge(ld[f"c{n}"], 16)
            transposes("w_cross", [wc_raw[:, n, :] for n in range(4)])
            pe.wait_ge(ld["ctx"], 16)
            transposes("ctx0", [ctx_tok[:, b, :] for b in range(HB)])
            transposes("ctx1", [ctx_tok[:, b, :] for b in range(HB, NB)])
            pe.wait_ge(out_a, out_count("ctx1", False))
            values("vc0", wc_t[:, 2, :], ctx_t, 0)
            values("vc1", wc_t[:, 2, :], ctx_t, 1)
            pe.wait_ge(ld["rw"], 16)
            transposes("w_router", [rw_raw[:, :]])
            pe.wait_ge(out_v, out_count("rel", True))
            for n in range(L // 4):
                start(f"bias{n}")
                if n % 8 == 0:
                    pe.wait_ge(spread_ready, n // 8 + 1)
                for m in range(4):
                    i = 4 * n + m
                    last = nc.tensor.matmul(bank_of(f"bias{n}")[:, m * 128:(m + 1) * 128],
                                            rel_t[:, L - 1 - i:2 * L - 1 - i], q_spread[:, i // 32 % 2, i % 32, :],
                                            start=True, stop=True)
                last.then_inc(task_done, 1)
            project("kc0", wc_t[:, 1, :], ctx_t, 0)
            project("kc1", wc_t[:, 1, :], ctx_t, 1)
            pe.wait_ge(out_v, sum(by_vector(t) for t in TASKS))
            pe.wait_ge(out_a, sum(not by_vector(t) for t in TASKS) - 2)
            pe.wait_ge(bank_zero, 1)
            pe.wait_ge(consts_made, 1)
            pe.wait_ge(pads_made, 4)

            def product(bank, w, act, first, last):
                for n, (a, b) in enumerate(((0, 0), (1, 0), (0, 1))):
                    ins = nc.tensor.matmul(bank, w[a], act[b], start=(first and n == 0), stop=(last and n == 2),
                                           skip_group_check=True)
                return ins

            def scores(U):
                B, g = U // NG, U % NG
                b, r, bank = B % NB, B % 2, ps[BS[U % 3]]
                if U == 2:
                    pe.wait_ge(out_a, sum(not by_vector(t) for t in TASKS))
                if U >= 3:
                    pe.wait_ge(exp_done, U - 2)
                if g == 0:
                    pe.wait_ge(qk_ready, 4 * (B + 1))
                if U < NU:
                    for h4 in range(GH):
                        row = (g * GH + h4) * NB + b
                        nc.tensor.matmul(bank[:, h4 * L:(h4 + 1) * L], pos[:, row, :], ident[:, :],
                                         start=(h4 == 0), stop=False, is_transpose=True, skip_group_check=True)
                else:
                    nc.tensor.matmul(bank[:, :].rearrange("p (h j) -> p h j", h=GH), identb[:, :],
                                     causal[:, :].unsqueeze(1).broadcast_to([128, GH, L]), start=True, stop=False,
                                     skip_group_check=True)
                last = product(bank[:, :], [q_bd[:, n, r, g, :] for n in range(2)],
                               [k_bd[:, n, r].rearrange("p h j -> p (h j)") for n in range(2)], False, True)
                last.then_inc(scores_ready, 1)

            def wait_probs(U):
                v, n = probs_copied(U)
                pe.wait_ge(pt_out_v if v else pt_out_a, n)

            def transpose_probs(U):
                pe.wait_ge(exp_done, U + 1)
                if U >= 1:
                    wait_probs(U - 1)
                for h4 in range(GH):
                    last = nc.tensor.transpose(ps[BP][:, h4 * L:(h4 + 1) * L],
                                               probs[:, U % 3, h4 * L:(h4 + 1) * L], ident[:, :])
                last.then_inc(probst_ready, 1)

            def values_of(U):
                B, g = U // NG, U % NG
                wait_probs(U)
                if g == 0 and B >= 1:
                    pe.wait_ge(ot_out, B)
                for h4 in range(GH):
                    last = nc.tensor.matmul(ps[BO][32 * h4:32 * h4 + NV, g * L:(g + 1) * L],
                                            v_aug[:, B // NB, B % NB, g * GH + h4, :],
                                            probs_t[:, U % 3, h4 * L:(h4 + 1) * L], start=True, stop=True)
                last.then_inc(pv_done, 1)

            def back(B):
                pe.wait_ge(ot_out, B + 1)
                if B >= 1:
                    pe.wait_ge(on_ready, B)
                for g in range(NG):
                    last = nc.tensor.transpose(ps[BM][:, g * 128:(g + 1) * 128], o_t[:, B % 2, g * 128:(g + 1) * 128],
                                               ident[:, :])
                last.then_inc(back_ready, 1)

            def turn_outputs(B):
                pe.wait_ge(on_ready, B + 1)
                if B >= 2:
                    pe.wait_ge(xt_out, B - 1)
                if NG * B + M + TURN > CT[0]:
                    pe.wait_ge(ct_out, 1)
                nc.tensor.transpose(ps[BN][:, 0:128], o_norm[:, B % 2, :], ident[:, :]).then_inc(ont_ready, 1)

            def read_tokens(B):
                pe.wait_ge(qc_out, B + 1) if B < NB else pe.wait_ge(logit_exp, B - NB + 1)

            def output_projection(B):
                pe.wait_ge(ont_out, B + 1)
                if B >= 1:
                    pe.wait_ge(mom_ready, B)
                if B >= 2:
                    read_tokens(B - 2)
                w = w_t[:, 3, :] if B < NB else wc_t[:, 3, :]
                nc.tensor.matmul(ps[BX][:, 0:D], on_t[:, B % 2, :], w, start=True, stop=True)\
                    .then_inc(proj_ready, 1)

            def turn_tokens(B):
                pe.wait_ge(x_norm, B + 1)
                src = (x1_tok if B < NB else x2_tok)[:, B % NB, :]
                pe.wait_ge(ont_out, min(B + 2, 2 * NB))
                if NG * B + M + TOKENS > CT[0]:
                    pe.wait_ge(ct_out, 1)
                nc.tensor.transpose(ps[BN][:, 0:D], src, ident[:, :]).then_inc(xt_ready, 1)

            def use_tokens(B):
                b = B % NB
                pe.wait_ge(xt_out, B + 1)
                pe.wait_ge(mom_ready, min(B + 2, 2 * NB))
                if B == 2 * NB - 1:
                    read_tokens(B - 1)
                if B < NB:
                    nc.tensor.matmul(ps[BX][:, 0:L], wc_t[:, 0, :], x1_t[:, b % 2, :], start=True, stop=True)\
                        .then_inc(q_ready, 1)
                else:
                    nc.tensor.matmul(ps[BX][:, 0:E], x2_t[:, b * L:(b + 1) * L], rw_t[:, :],
                                     start=True, stop=True).then_inc(logit_ready, 1)

            def turn_weights(f):
                pe.wait_ge(comb_ready, f + 2)
                pe.wait_ge(ont_out, min((CT[f] - M - TURN) // NG + 1, 2 * NB))
                pe.wait_ge(xt_out, min((CT[f] - M - TOKENS) // NG + 1, 2 * NB))
                for n in range(HB):
                    last = nc.tensor.transpose(ps[BN][:, n * 64:(n + 1) * 64].bitcast(F16),
                                               comb_split[:, n, :, :].rearrange("p s e -> p (s e)"), ident_h[:, :])
                last.then_inc(ct_ready, 1)

            def expert_up(k):
                f, c = k // CH, k % CH - NSH
                if k >= 2:
                    pe.wait_ge(relu_ready, k - 1)
                if c == -NSH:
                    pe.wait_ge(x2_split, (f + 1) * HB)
                if k == 0:
                    wait_split(pe, NB - 1)
                    pe.wait_ge(exp_done, STAGES)
                if c >= 0:
                    w = [t[:, 0, c * 128:(c + 1) * 128] for t in (w_hi, w_lo)]
                else:
                    w = [t[:, 0, (c + NSH) * 128:(c + NSH + 1) * 128] for t in (sh_hi, sh_lo)]
                product(ps[BH[k % 2]][:, :], w, [t[:, f * HT:(f + 1) * HT] for t in (x2_hi, x2_lo)],
                        True, True).then_inc(h_ready, 1)

            def spread_weights(k):
                f, c = k // CH, k % CH - NSH
                if c >= 0:
                    n = f * NPAIR + c
                    if n >= 2:
                        pe.wait_ge(unit_ready, k - 1 if c >= 2 else k - 1 - NSH)
                    if c == 0:
                        pe.wait_ge(ct_out, f + 1)
                    if n == 0:
                        wait_probs(STAGES - 1)
                        pe.wait_ge(consts_made, 4 + NB)
                    nc.tensor.matmul(ps[BC[n % 2]][:, :], select[:, c].rearrange("p e i -> p (e i)"),
                                     comb_t[:, f * HT:(f + 1) * HT], start=True, stop=True).then_inc(c_ready, 1)

            def expert_down(k):
                f, c = k // CH, k % CH - NSH
                pe.wait_ge(lo_ready, k + 1)
                if k == 0:
                    pe.wait_ge(ot_out, 2 * NB)
                if k == CH:
                    pe.wait_ge(ct_out, 2)
                if c >= 0:
                    w = [t[:, 1, c * 128:(c + 1) * 128] for t in (w_hi, w_lo)]
                else:
                    w = [t[:, 1, (c + NSH) * 128:(c + NSH + 1) * 128] for t in (sh_hi, sh_lo)]
                product(ps[(BO, BN)[f]][:, :], w, (unit_hi[:, k % R], unit_lo[:, k % R]), c == -NSH,
                        c == NPAIR - 1).then_inc(down_done, 1)

            def turn_y(f):
                pe.wait_ge(y_out_t, f + 1)
                if f == 0:
                    pe.wait_ge(on_ready, 2 * NB)
                else:
                    pe.wait_ge(ymom_ready, 1)
                for n in range(HB):
                    last = nc.tensor.transpose(ps[BM][:, n * D:(n + 1) * D], y_t[:, n * L:(n + 1) * L], ident[:, :])
                last.then_inc(yback_ready, 1)

            for s in range(STEPS):
                k = s - MOE0
                if s < STAGES:
                    scores(s)
                if 0 <= k < 2 * CH:
                    expert_up(k)
                if s in CT:
                    turn_weights(CT.index(s))
                if 0 <= k < 2 * CH:
                    spread_weights(k)
                for m, part in ((M + BACK, back), (M + TURN, turn_outputs), (M + PROJ, output_projection),
                                (M + TOKENS, turn_tokens), (M + USE, use_tokens)):
                    if (s - m) % NG == 0 and 0 <= (s - m) // NG < 2 * NB:
                        part((s - m) // NG)
                if 0 <= s - LT < STAGES:
                    transpose_probs(s - LT)
                if 0 <= s - LV < STAGES:
                    values_of(s - LV)
                if k == CH + LD + 2:
                    turn_y(0)
                if LD <= k:
                    expert_down(k - LD)
            turn_y(1)

        @block.scalar
        def _(act):
            chain = [0]

            def link(ins):
                chain[0] += 1
                ins.then_inc(a_chain, 1)
                act.wait_ge(a_chain, chain[0])

            act.preload_act_table_set("natural_log_exp_and_others")

            def done(task):
                act.wait_ge(task_done, TASKS.index(task) + 1)
                return bank_of(task)[:, :]

            nc.scalar.copy(x_t[:, 0:HT], done("x0")).then_inc(out_a, 1)
            nc.scalar.copy(x_t[:, HT:], done("x1")).then_inc(out_a, 1)
            act.wait_ge(ld["qkvb"], 16)
            nc.scalar.activation(q_t[:, 0:HT], done("q0"), ACT.Identity, bias=qkvb_col[:, 0:1]).then_inc(out_a, 1)
            nc.scalar.activation(q_t[:, HT:], done("q1"), ACT.Identity, bias=qkvb_col[:, 0:1]).then_inc(out_a, 1)
            link(nc.scalar.mul(kb_col[:, :], qkvb_col[:, 1:2], SCALE))
            for f in range(2):
                nc.scalar.activation(k_t[:, f * HT:(f + 1) * HT], done(f"k{f}"), ACT.Identity, bias=kb_col[:, :],
                                     scale=SCALE).then_inc(out_a, 1)
            nc.scalar.copy(wc_t[:, :, :].rearrange("p c d -> p (c d)"), done("w_cross")).then_inc(out_a, 1)
            nc.scalar.copy(ctx_t[:, 0:HT], done("ctx0")).then_inc(out_a, 1)
            nc.scalar.copy(ctx_t[:, HT:], done("ctx1")).then_inc(out_a, 1)
            for f in range(2):
                nc.scalar.copy(v_aug[:, 1, f * HB:(f + 1) * HB, :, 0:HD].rearrange("p b h d -> p (b h) d"),
                               done(f"vc{f}").rearrange("p (n d) -> p n d", d=HD)).then_inc(out_a, 1)
            nc.scalar.copy(rw_t[:, :], done("w_router")[:, 0:E]).then_inc(out_a, 1)
            for n in range(L // 4):
                if not by_vector(f"bias{n}"):
                    nc.scalar.copy(pos[:, :, 4 * n:4 * n + 4],
                                   done(f"bias{n}").rearrange("p (i r) -> p r i", i=4)).then_inc(out_a, 1)
            nc.scalar.mul(kc_t[:, 0:HT], done("kc0"), SCALE).then_inc(out_a, 1)
            nc.scalar.mul(kc_t[:, HT:], done("kc1"), SCALE).then_inc(out_a, 1)
            act.wait_ge(consts_made, 4)

            def exps(U):
                act.wait_ge(max_ready, U + 1)
                if U >= 3:
                    act.wait_ge(probst_ready, U - 2)
                for h4 in range(GH):
                    last = nc.scalar.activation(probs[:, U % 3, h4 * L:(h4 + 1) * L],
                                                ps[BS[U % 3]][:, h4 * L:(h4 + 1) * L], ACT.Exp,
                                                bias=neg_max[:, U % 4, h4:h4 + 1])
                last.then_inc(exp_done, 1)

            def probs_out(U):
                act.wait_ge(probst_ready, U + 1)
                if U >= 3:
                    act.wait_ge(pv_done, U - 2)
                nc.scalar.copy(probs_t[:, U % 3, :], ps[BP][:, :]).then_inc(pt_out_a, 1)

            def outputs_out(B):
                act.wait_ge(pv_done, NG * (B + 1))
                if B >= 2:
                    act.wait_ge(back_ready, B - 1)
                nc.scalar.copy(o_t[:, B % 2, :], ps[BO][:, :]).then_inc(ot_out, 1)

            def turned_out(B):
                act.wait_ge(ont_ready, B + 1)
                if B >= 2:
                    act.wait_ge(proj_ready, B - 1)
                nc.scalar.copy(on_t[:, B % 2, :], ps[BN][:, 0:128]).then_inc(ont_out, 1)

            def deviation(B):
                act.wait_ge(mom_ready, B + 1)
                link(nc.scalar.activation(ln_var[:, B % 2], moments[:, B % 2, 1:2], ACT.Ln, bias=eps_col[:, :]))
                nc.scalar.activation(rstd[:, B % 2], ln_var[:, B % 2], ACT.Exp, scale=-0.5).then_inc(rstd_ready, 1)

            def tokens_out(B):
                act.wait_ge(xt_ready, B + 1)
                b = B % NB
                if 2 <= B < NB:
                    act.wait_ge(q_ready, B - 1)
                if B == NB:
                    act.wait_ge(task_done, len(TASKS))
                dst = x1_t[:, b % 2, :] if B < NB else x2_t[:, b * L:(b + 1) * L]
                if B >= NB:
                    nc.scalar.copy(x2_hi[:, b * L:(b + 1) * L], ps[BN][:, 0:D])
                nc.scalar.copy(dst, ps[BN][:, 0:D]).then_inc(xt_out, 1)

            def queries_out(B):
                b = B % NB
                if B < NB:
                    act.wait_ge(q_ready, b + 1)
                    act.wait_ge(qk_ready, 4 * (b + 1))
                    nc.scalar.activation(q_hi[:, b * L:(b + 1) * L].bitcast(F32R), ps[BX][:, 0:L], ACT.Identity)
                    nc.scalar.copy(qc_t[:, b * L:(b + 1) * L], ps[BX][:, 0:L]).then_inc(qc_out, 1)
                else:
                    act.wait_ge(logit_ready, b + 1)
                    if b in (HB, HB + 2):
                        act.wait_ge(exp_read, (b - HB) // 2 + 1)
                    nc.scalar.activation(r_exp[:, b % HB, :], ps[BX][:, 0:E], ACT.Exp, scale=-1.0)\
                        .then_inc(logit_exp, 1)

            def weights_out(f):
                act.wait_ge(ct_ready, f + 1)
                nc.scalar.copy(comb_t[:, f * HT:(f + 1) * HT], ps[BN][:, 0:HT // 2].bitcast(F16)).then_inc(ct_out, 1)

            def squares(k):
                act.wait_ge(h_ready, k + 1)
                if k == 0:
                    wait_split(act, NB - 1)
                else:
                    act.wait_ge(sq_ready, k)
                nc.scalar.activation(relu_sb[:, :], ps[BH[k % 2]][:, :], ACT.Relu).then_inc(relu_ready, 1)
                if k >= 2:
                    act.wait_ge(unit_ready, k - 1)
                act.wait_ge(relu_ready, k + 1)
                nc.scalar.activation(sq[:, k % 2], relu_sb[:, :], ACT.Square).then_inc(sq_ready, 1)

            def y_copy(f):
                act.wait_ge(down_done, (f + 1) * CH)
                if f == 1:
                    act.wait_ge(yback_ready, 1)
                nc.scalar.copy(y_t[:, :], ps[(BO, BN)[f]][:, :]).then_inc(y_out_t, 1)

            def y_deviation(f):
                act.wait_ge(ymom_ready, f + 1)
                link(nc.scalar.activation(y_ln[:, :], y_mom[:, :, 1], ACT.Ln, bias=eps_col[:, :]))
                nc.scalar.activation(y_rstd[:, :], y_ln[:, :], ACT.Exp, scale=-0.5).then_inc(yrstd_ready, 1)

            for s in range(STEPS):
                k = s - MOE0
                for m, part in ((M - 1, outputs_out), (M + TURN + 1, turned_out), (M + TOKENS + 1, tokens_out),
                                (M + USE + 1, queries_out)):
                    if (s - m) % NG == 0 and 0 <= (s - m) // NG < 2 * NB:
                        part((s - m) // NG)
                if s in CT:
                    weights_out(CT.index(s))
                if 0 <= s - LT < STAGES and not probs_by_vector(s - LT):
                    probs_out(s - LT)
                if s < STAGES:
                    exps(s)
                if 0 <= k < 2 * CH:
                    squares(k)
                if (s - M - PROJ - 1) % NG == 0 and 0 <= (s - M - PROJ - 1) // NG < 2 * NB:
                    deviation((s - M - PROJ - 1) // NG)
                if k == CH + LD:
                    y_copy(0)
                if k == CH + LD + 5:
                    y_deviation(0)
            y_copy(1)
            y_deviation(1)

        @block.vector
        def _(dve):
            chain = [0]

            def link(ins):
                chain[0] += 1
                ins.then_inc(v_chain, 1)
                dve.wait_ge(v_chain, chain[0])

            def mark(ins):
                chain[0] += 1
                ins.then_inc(v_chain, 1)

            def settle():
                if chain[0]:
                    dve.wait_ge(v_chain, chain[0])

            def done(task):
                dve.wait_ge(task_done, TASKS.index(task) + 1)
                return bank_of(task)[:, :]

            nc.vector.memset(ps[BO][:, :], 0.0).then_inc(bank_zero, 1)
            dve.wait_ge(masks_made, 1)
            nc.vector.tensor_reduce(slot_mask[:, :], head_mask[:, :].rearrange("p (g h) -> p h g", g=NG),
                                    AX.X, ALU.add).then_inc(groups_made, 1)
            nc.vector.tensor_reduce(group_mask[:, :], head_mask[:, :].rearrange("p (g h) -> p g h", g=NG),
                                    AX.X, ALU.add).then_inc(groups_made, 1)
            nc.vector.tensor_copy(w_t[:, :, :].rearrange("p c d -> p (c d)"), done("w_self")).then_inc(out_v, 1)
            dve.wait_ge(pads_made, 3)
            nc.vector.tensor_copy(rel_t[:, REL0:REL0 + NREL], done("rel")[:, 0:NREL]).then_inc(out_v, 1)

            def spread_queries(c):
                if c >= 2:
                    dve.wait_ge(task_done, TASKS.index(f"bias{8 * (c - 1) - 1}") + 1)
                src = q_t[:, 32 * NB * c:32 * NB * (c + 1)].rearrange("p (i b) -> p i b", b=NB)
                for h in range(H):
                    last = nc.vector.tensor_scalar(q_spread[:, c % 2, :, h * NB:(h + 1) * NB], src,
                                                   head_mask[:, h:h + 1], None, ALU.mult)
                last.then_inc(spread_ready, 1)

            def split_heads(hi, t, cols):
                link(nc.vector.tensor_copy(hi[:, cols].bitcast(F32R), t[:, cols]))
                return nc.vector.tensor_tensor(t[:, cols], t[:, cols], hi[:, cols], ALU.subtract)

            def values_out(half):
                nc.vector.tensor_tensor(v_aug[:, 0, half * HB:(half + 1) * HB, :, 0:HD],
                                        done(f"v{half}").rearrange("p (b h d) -> p b h d", b=HB, h=H),
                                        vb_row[:, :].rearrange("p (h d) -> p h d", h=H).unsqueeze(1)
                                        .broadcast_to([128, HB, H, HD]), ALU.add).then_inc(out_v, 1)

            def bias_out(n):
                nc.vector.tensor_tensor(pos[:, :, 4 * n:4 * n + 4], done(f"bias{n}").rearrange("p (i r) -> p r i", i=4),
                                        rel_mask[:, 4 * n:4 * n + 4].unsqueeze(1).broadcast_to([128, H * NB, 4]),
                                        ALU.add).then_inc(out_v, 1)

            dve.wait_ge(out_a, out_count("q0", False))
            spread_queries(0)
            dve.wait_ge(ld["vb"], 16)
            values_out(0)
            values_out(1)
            spread_queries(1)
            dve.wait_ge(masks_made, 2)
            for n in range(L // 4):
                if n == 7:
                    dve.wait_ge(out_a, out_count("q1", False))
                if n in (7, 16):
                    spread_queries(2 + (n > 8))
                if n == 10:
                    dve.wait_ge(out_a, out_count("k1", False))
                    split_heads(k_hi, k_t, slice(0, NB * L)).then_inc(heads_split, 1)
                if n == 17:
                    dve.wait_ge(spread_ready, 4)
                    split_heads(q_hi, q_t, slice(0, NB * L)).then_inc(heads_split, 1)
                if by_vector(f"bias{n}"):
                    bias_out(n)

            def maxima(U):
                dve.wait_ge(scores_ready, U + 1)
                if U >= 4:
                    dve.wait_ge(exp_done, U - 3)
                nc.vector.tensor_reduce(neg_max[:, U % 4, :], ps[BS[U % 3]][:, :].rearrange("p (h j) -> p h j", h=GH),
                                        AX.X, ALU.max, negate=True).then_inc(max_ready, 1)

            def probs_out(U):
                dve.wait_ge(probst_ready, U + 1)
                if U >= 3:
                    dve.wait_ge(pv_done, U - 2)
                nc.vector.tensor_copy(probs_t[:, U % 3, :], ps[BP][:, :]).then_inc(pt_out_v, 1)

            def normalise(B):
                dve.wait_ge(back_ready, B + 1)
                if B >= 2:
                    dve.wait_ge(ont_ready, B - 1)
                o = ps[BM][:, :].rearrange("p (h c) -> p h c", h=H)
                link(nc.vector.reciprocal(rden[:, B % 2, :], o[:, :, HD]))
                nc.vector.tensor_tensor(o_norm[:, B % 2, :].rearrange("p (h d) -> p h d", h=H), o[:, :, 0:HD],
                                        rden[:, B % 2, :].unsqueeze(2).broadcast_to([128, H, HD]), ALU.mult)\
                    .then_inc(on_ready, 1)

            def residual(B):
                dve.wait_ge(proj_ready, B + 1)
                if B == 0:
                    dve.wait_ge(xb_made, 1)
                base = (x_tok if B < NB else x1_tok)[:, B % NB, :]
                link(nc.vector.tensor_tensor(res[:, B % 2, :], ps[BX][:, 0:D], base, ALU.add))
                link(nc.vector.bn_stats(stats[:, B % 2, :], res[:, B % 2, :]))
                nc.vector.bn_aggr(moments[:, B % 2, :], stats[:, B % 2, :]).then_inc(mom_ready, 1)

            def layer_norm(B):
                dve.wait_ge(rstd_ready, B + 1)
                dst = (x1_tok if B < NB else x2_tok)[:, B % NB, :]
                nc.vector.tensor_scalar(dst, res[:, B % 2, :], moments[:, B % 2, 0:1], rstd[:, B % 2, :],
                                        ALU.subtract, ALU.mult).then_inc(x_norm, 1)

            def route(q, part):
                seqs = BATCHES[q][0]
                size, first = len(seqs), seqs[0] % HB
                all_n = slice(first, first + size)
                settle()
                if part == 0:
                    dve.wait_ge(logit_exp, seqs[-1] + 1)
                    dve.wait_ge(ld["corr"], 16)
                    nc.vector.tensor_scalar(r_one[:, all_n, :], r_exp[:, all_n, :], 1.0, None, ALU.add)\
                        .then_inc(exp_read, 1)
                    dve.wait_ge(exp_read, q + 1)
                    mark(nc.vector.reciprocal(score[:, all_n, :], r_one[:, all_n, :]))
                if part == 1:
                    mark(nc.vector.tensor_tensor(biased[:, all_n, :], score[:, all_n, :],
                                                 corr_row[:, :].unsqueeze(1).broadcast_to([128, size, E]), ALU.add))
                if 2 <= part < 6:
                    members = range(first + (part - 2) * size // 4, first + (part - 1) * size // 4)
                    for n in members:
                        for g in range(EG):
                            last = nc.vector.max(top_in[:, n, g, :], biased[:, n, g * ES:(g + 1) * ES])
                    if members:
                        mark(last)
                if part == 6:
                    link(nc.vector.tensor_tensor(gscore[:, all_n, 0:EG],
                                                 top_in[:, all_n, :, 0], top_in[:, all_n, :, 1], ALU.add))
                    for n in range(first, first + size):
                        last = nc.vector.max(gtop[:, n, :], gscore[:, n, 0:EG])
                    link(last)
                    mark(nc.vector.tensor_copy(glist[:, all_n, 0:TOPG], gtop[:, all_n, 0:TOPG]))
                if part == 7:
                    for n in range(first, first + size):
                        last = nc.vector.match_replace(grep[:, n, :], glist[:, n, :], gscore[:, n, :], 3.0e38)
                    mark(last)
                if part == 8:
                    link(nc.vector.tensor_tensor(gkeep[:, all_n, :], grep[:, all_n, 0:EG],
                                                 gscore[:, all_n, 0:EG], ALU.not_equal))
                    mark(nc.vector.tensor_tensor(
                        masked[:, all_n, :].rearrange("p n (g e) -> p (n g) e", g=EG),
                        biased[:, all_n, :].rearrange("p n (g e) -> p (n g) e", g=EG),
                        gkeep[:, all_n, :].rearrange("p n g -> p (n g)").unsqueeze(2)
                        .broadcast_to([128, size * EG, ES]),
                        ALU.mult))
                if part == 9:
                    for n in range(first, first + size):
                        last = nc.vector.max(etop[:, n, :], masked[:, n, :])
                    mark(last)
                if part == 10:
                    for n in range(first, first + size):
                        last = nc.vector.match_replace(erep[:, n, :], etop[:, n, :], masked[:, n, :], 3.0e38)
                    link(last)
                    mark(nc.vector.tensor_tensor(chosen[:, all_n, :], erep[:, all_n, :], masked[:, all_n, :],
                                                 ALU.not_equal))
                if part == 11:
                    link(nc.vector.tensor_tensor(weight[:, all_n, :], score[:, all_n, :], chosen[:, all_n, :],
                                                 ALU.mult))
                    link(nc.vector.tensor_reduce(wsum[:, all_n], weight[:, all_n, :], AX.X, ALU.add))
                    link(nc.vector.tensor_scalar(wsum1[:, all_n], wsum[:, all_n], 1e-20, None, ALU.add))
                    mark(nc.vector.reciprocal(wrec[:, all_n], wsum1[:, all_n]))
                if part == 12:
                    if q >= 2:
                        dve.wait_ge(ct_ready, 1)
                    for n in range(first, first + size):
                        last = nc.vector.tensor_scalar(comb[:, n, :], weight[:, n, :], wrec[:, n:n + 1], ROUTE_SCALE,
                                                       ALU.mult, ALU.mult)
                    mark(last)
                if part == 13:
                    link(nc.vector.tensor_copy(comb_split[:, all_n, 0, :], comb[:, all_n, :]))
                    link(nc.vector.tensor_tensor(comb_rest[:, all_n, :], comb[:, all_n, :], comb_split[:, all_n, 0, :],
                                                 ALU.subtract))
                    nc.vector.tensor_scalar(comb_split[:, all_n, 1, :], comb_rest[:, all_n, :], LO, None, ALU.mult)\
                        .then_inc(comb_ready, 1)

            def split_weights(n):
                dve.wait_ge(w_high, n + 1)
                if n == 0:
                    dve.wait_ge(shared_high, 1)
                    nc.vector.tensor_tensor(sh_lo[:, :, :], shared[:, :, :], sh_hi[:, :, :], ALU.subtract)
                way, cols = piece(n)
                nc.vector.tensor_tensor(w_lo[:, way, cols], incoming[:, n % 2], w_hi[:, way, cols],
                                        ALU.subtract).then_inc(w_split_v, 1)

            def units(k):
                f, c = k // CH, k % CH - NSH
                dve.wait_ge(sq_ready, k + 1)
                if k >= 3:
                    dve.wait_ge(lo_ready, k - 2)
                if c >= 0:
                    n = f * NPAIR + c
                    dve.wait_ge(c_ready, n + 1)
                    ins = nc.vector.tensor_tensor(unit[:, k % 3], ps[BC[n % 2]][:, :], sq[:, k % 2], ALU.mult)
                else:
                    ins = nc.vector.tensor_copy(unit[:, k % 3], sq[:, k % 2])
                ins.then_inc(unit_ready, 1)

            def units_high(k):
                dve.wait_ge(unit_ready, k + 1)
                if k >= R:
                    dve.wait_ge(down_done, k - R + 1)
                nc.vector.tensor_copy(unit_hi[:, k % R], unit[:, k % 3]).then_inc(hi_ready, 1)

            def y_residual(f, part):
                if part == 1:
                    for n in range(HB):
                        last = nc.vector.bn_stats(y_stats[:, n, :], y_res[:, n, :])
                    link(last)
                    for n in range(HB):
                        last = nc.vector.bn_aggr(y_mom[:, n, :], y_stats[:, n, :])
                    last.then_inc(ymom_ready, 1)
                    return
                dve.wait_ge(yback_ready, f + 1)
                if f:
                    dve.wait_ge(yrstd_ready, 1)
                link(nc.vector.tensor_tensor(y_res[:, :, :].rearrange("p n d -> p (n d)"), ps[BM][:, :],
                                             x2_tok[:, f * HB:(f + 1) * HB, :].rearrange("p n d -> p (n d)"), ALU.add))

            def y_norm(f):
                dve.wait_ge(yrstd_ready, f + 1)
                for n in range(HB):
                    last = nc.vector.tensor_scalar(y_out[:, f * HB + n, :], y_res[:, n, :], y_mom[:, n, 0:1],
                                                   y_rstd[:, n:n + 1], ALU.subtract, ALU.mult)
                last.then_inc(y_done, 1)

            for s in range(STEPS):
                k = s - MOE0
                for m, part in ((M + BACK + 1, normalise), (M + PROJ + 1, residual), (M + NORM, layer_norm)):
                    if (s - m) % NG == 0 and 0 <= (s - m) // NG < 2 * NB:
                        part((s - m) // NG)
                if s < STAGES:
                    maxima(s)
                if 0 <= s - LT < STAGES and probs_by_vector(s - LT):
                    probs_out(s - LT)
                if 0 <= k < 2 * CH:
                    units(k)
                for q, (_, rate) in enumerate(BATCHES):
                    for part in range(PARTS):
                        if s - ROUTE0[q] == int(part / rate):
                            route(q, part)
                if s == 2:
                    split_heads(kc_hi, kc_t, slice(0, NB * L)).then_inc(heads_split, 1)
                if (s - M - USE - 3) % NG == 0 and 0 <= (s - M - USE - 3) // NG < NB:
                    b = (s - M - USE - 3) // NG
                    dve.wait_ge(qc_out, b + 1)
                    nc.vector.tensor_tensor(q_t[:, b * L:(b + 1) * L], q_t[:, b * L:(b + 1) * L],
                                            q_hi[:, b * L:(b + 1) * L], ALU.subtract).then_inc(qc_split, 1)
                if (s - NG * NB - 2) % NG == 0 and 0 <= (s - NG * NB - 2) // NG < BY_POOL:
                    split_weights((s - NG * NB - 2) // NG)
                if k == CH + LD + 3:
                    y_residual(0, 0)
                if k == CH + LD + 4:
                    y_residual(0, 1)
                if k == CH + LD + 6:
                    y_norm(0)
                if 0 <= k < 2 * CH:
                    units_high(k)
            y_residual(1, 0)
            y_residual(1, 1)
            y_norm(1)


_INS = ["x", "ctx_1024", "L0_attn_qkv_w", "L0_attn_qkv_b", "L0_attn_proj_w", "L0_attn_proj_b", "L0_attn_rel_emb",
        "L0_xattn_wq", "L0_xattn_wk", "L0_xattn_wv", "L0_xattn_wo", "L0_ffn_router_w", "L0_ffn_correction_bias",
        "L0_ffn_up_w", "L0_ffn_down_w", "L0_ffn_shared_up_w", "L0_ffn_shared_down_w"]


def kernel(**inputs):
    import numpy as _np
    import concourse.bacc as _bacc
    from concourse import mybir as _mybir
    from concourse.bass_utils import run_bass_kernel_spmd as _run

    nc = _bacc.Bacc("TRN2", target_bir_lowering=False, num_devices=1)
    arrays, args = {}, []
    for name in _INS:
        a = _np.ascontiguousarray(inputs[name])
        arrays[f"in_{name}"] = a
        args.append(nc.dram_tensor(f"in_{name}", a.shape, _mybir.dt.from_np(a.dtype), kind="ExternalInput").ap())
    args.append(nc.dram_tensor("out_0", (NB, L, D), F32, kind="ExternalOutput").ap())
    decoder_layer(nc, *args)
    r = _run(nc, [arrays], core_ids=[0])
    return r.results[0]["out_0"]
```
